# Optimizing a Trainium2 kernel written in Bass

```python
import numpy as np
import jax
import jax.numpy as jnp

def _softmax(x, axis=-1):
    return jax.nn.softmax(x, axis=axis)

def _gelu(x):
    return jax.nn.gelu(x, approximate=True)

def _silu(x):
    return jax.nn.silu(x)

def _sigmoid(x):
    return jax.nn.sigmoid(x)

def _layernorm(x, axis=-1, eps=1e-05):
    m = jnp.mean(x, axis=axis, keepdims=True)
    v = jnp.var(x, axis=axis, keepdims=True)
    return (x - m) / jnp.sqrt(v + eps)

def _scatter_add(tgt, idx, src, axis=0):
    return tgt.at[idx].add(src)

def _segment_sum(src, seg, n):
    return jax.ops.segment_sum(src, seg, n)
kernel_name = 'mk_adj_preln_d4_adj_r2_93b44c'

def setup_inputs(seed: int=0):
    np.random.seed(seed)
    _w = jnp.asarray

    def _rec_inputs():
        import jax
        import jax.numpy as jnp
        _gk = jax.random.key(seed)
        x = -0.0002928 + 1 * jax.random.normal(jax.random.fold_in(_gk, 1), (128, 128, 128), jnp.float32)
        _a = jax.random.bernoulli(jax.random.fold_in(_gk, 2), 0.03125, (128, 128, 128))
        _a = jnp.logical_or(_a, jnp.swapaxes(_a, -1, -2))
        _a = jnp.logical_or(_a, jnp.eye(128, dtype=bool))
        _af = _a.astype(jnp.float32)
        _af = _af * jax.random.uniform(jax.random.fold_in(_gk, 3), (128, 128, 128), jnp.float32, 0.05, 1)
        adj = _af
        return (x, adj)
    x, adj = _rec_inputs()

    def _L0_gnn_setup():
        import jax, jax.numpy as jnp
        import numpy as np
        B, N, F_IN, F_OUT = (8, 1024, 128, 128)
        key = jax.random.key(seed)
        k1, k2, k3, k4 = jax.random.split(key, 4)
        x = jax.random.normal(k1, (B, N, F_IN), dtype=jnp.float32)
        adj = jax.random.uniform(k2, (B, N, N), dtype=jnp.float32)
        W = jax.random.normal(k3, (F_IN, F_OUT), dtype=jnp.float32) * (1.0 / np.sqrt(F_IN))
        b = jax.random.normal(k4, (F_OUT,), dtype=jnp.float32)
        return {'x': x, 'adj': adj, 'W': W, 'b': b}
    _L0_gnn_all = _L0_gnn_setup()
    _L0_gnn_in = {k: v for k, v in _L0_gnn_all.items() if k in ('W', 'b')}
    del _L0_gnn_all

    def _L1_gnn_setup():
        import jax, jax.numpy as jnp
        import numpy as np
        from jax import lax
        DIM = 128
        EPS = 1e-05

        def _bn(h, g, b, m, v):
            scale = g / jnp.sqrt(v + EPS)
            return h * scale[None, :, None] + (b - m * scale)[None, :, None]

        def _conv1d(h, w, pad):
            return lax.conv_general_dilated(h, w, window_strides=(1,), padding=[(pad, pad)], dimension_numbers=('NCH', 'OIH', 'NCH'))
        key = jax.random.key(seed)
        ks = jax.random.split(key, 16)
        bs, n, d = (16, 1024, DIM)
        s = 0.05
        return {'x': jax.random.normal(ks[0], (bs, n, d), jnp.float32), 'mask': jnp.ones((bs, n, n), jnp.float32), 'w_se': jax.random.normal(ks[1], (3, d), jnp.float32) * s, 'b_se': jnp.zeros((3,), jnp.float32), 'conv1_w': jax.random.normal(ks[2], (d, d, 1), jnp.float32) * s, 'bn1_g': jnp.ones((d,), jnp.float32), 'bn1_b': jnp.zeros((d,), jnp.float32), 'bn1_m': jnp.zeros((d,), jnp.float32), 'bn1_v': jnp.ones((d,), jnp.float32), 'conv2_w': jax.random.normal(ks[3], (d, d, 17), jnp.float32) * s, 'bn2_g': jnp.ones((d,), jnp.float32), 'bn2_b': jnp.zeros((d,), jnp.float32), 'bn2_m': jnp.zeros((d,), jnp.float32), 'bn2_v': jnp.ones((d,), jnp.float32), 'w_msg': jax.random.normal(ks[4], (d, d), jnp.float32) * s, 'b_msg': jnp.zeros((d,), jnp.float32), 'w_ih': jax.random.normal(ks[5], (3 * d, 2 * d), jnp.float32) * s, 'b_ih': jnp.zeros((3 * d,), jnp.float32), 'w_hh': jax.random.normal(ks[6], (3 * d, d), jnp.float32) * s, 'b_hh': jnp.zeros((3 * d,), jnp.float32)}
    _L1_gnn_all = _L1_gnn_setup()
    _L1_gnn_in = {k: v for k, v in _L1_gnn_all.items() if k in ('w_se', 'b_se', 'conv1_w', 'bn1_g', 'bn1_b', 'bn1_m', 'bn1_v', 'conv2_w', 'bn2_g', 'bn2_b', 'bn2_m', 'bn2_v', 'w_msg', 'b_msg', 'w_ih', 'b_ih', 'w_hh', 'b_hh')}
    del _L1_gnn_all

    def _L2_gnn_setup():
        import jax, jax.numpy as jnp
        import numpy as np
        H = 128
        EPS_RENORM = 1e-10
        EPS_LN = 1e-12
        key = jax.random.key(seed)
        ks = jax.random.split(key, 10)
        B, N = (8, 1024)
        hidden_state = jax.random.normal(ks[0], (B, N, H), dtype=jnp.float32)
        adjacency_matrix = jax.random.randint(ks[1], (B, N, N), 0, 2).astype(jnp.float32)

        def lin(kw, kb):
            W = jax.random.normal(kw, (H, H), dtype=jnp.float32) * (2.0 / (H + H)) ** 0.5
            bound = 1.0 / np.sqrt(H)
            b = jax.random.uniform(kb, (H,), minval=-bound, maxval=bound, dtype=jnp.float32)
            return (W, b)
        Wl, bl = lin(ks[2], ks[3])
        Ws, bs = lin(ks[4], ks[5])
        Wr, br = lin(ks[6], ks[7])
        ln_w = jnp.ones((H,), dtype=jnp.float32)
        ln_b = jnp.zeros((H,), dtype=jnp.float32)
        return {'hidden_state': hidden_state, 'adjacency_matrix': adjacency_matrix, 'Wl': Wl, 'bl': bl, 'Ws': Ws, 'bs': bs, 'Wr': Wr, 'br': br, 'ln_w': ln_w, 'ln_b': ln_b}
    _L2_gnn_all = _L2_gnn_setup()
    _L2_gnn_in = {k: v for k, v in _L2_gnn_all.items() if k in ('Wl', 'bl', 'Ws', 'bs', 'Wr', 'br', 'ln_w', 'ln_b')}
    del _L2_gnn_all

    def _L3_gnn_setup():
        import jax, jax.numpy as jnp
        import numpy as np
        B, N, D = (4, 2048, 128)
        DENSITY = 0.02
        key = jax.random.key(seed)
        kx, ka1, ka2, kwt, kbt, kwh, kth = jax.random.split(key, 7)
        x = jax.random.normal(kx, (B, N, D), dtype=jnp.float32)
        mask = jax.random.uniform(ka1, (B, N, N)) < DENSITY
        vals = jax.random.uniform(ka2, (B, N, N), dtype=jnp.float32)
        adj = jnp.where(mask, vals, 0.0).astype(jnp.float32)
        s = 0.02
        W_t = s * jax.random.normal(kwt, (D, D), dtype=jnp.float32)
        b_t = s * jax.random.normal(kbt, (D,), dtype=jnp.float32)
        W_h = s * jax.random.normal(kwh, (D, D), dtype=jnp.float32)
        theta = s * jax.random.normal(kth, (D, D), dtype=jnp.float32)
        return {'x': x, 'adj': adj, 'W_t': W_t, 'b_t': b_t, 'W_h': W_h, 'theta': theta}
    _L3_gnn_all = _L3_gnn_setup()
    _L3_gnn_in = {k: v for k, v in _L3_gnn_all.items() if k in ('W_t', 'b_t', 'W_h', 'theta')}
    del _L3_gnn_all
    return {'x': x, 'adj': adj, 'L0_gnn_W': _L0_gnn_in['W'], 'L0_gnn_b': _L0_gnn_in['b'], 'L1_gnn_w_se': _L1_gnn_in['w_se'], 'L1_gnn_b_se': _L1_gnn_in['b_se'], 'L1_gnn_conv1_w': _L1_gnn_in['conv1_w'], 'L1_gnn_bn1_g': _L1_gnn_in['bn1_g'], 'L1_gnn_bn1_b': _L1_gnn_in['bn1_b'], 'L1_gnn_bn1_m': _L1_gnn_in['bn1_m'], 'L1_gnn_bn1_v': _L1_gnn_in['bn1_v'], 'L1_gnn_conv2_w': _L1_gnn_in['conv2_w'], 'L1_gnn_bn2_g': _L1_gnn_in['bn2_g'], 'L1_gnn_bn2_b': _L1_gnn_in['bn2_b'], 'L1_gnn_bn2_m': _L1_gnn_in['bn2_m'], 'L1_gnn_bn2_v': _L1_gnn_in['bn2_v'], 'L1_gnn_w_msg': _L1_gnn_in['w_msg'], 'L1_gnn_b_msg': _L1_gnn_in['b_msg'], 'L1_gnn_w_ih': _L1_gnn_in['w_ih'], 'L1_gnn_b_ih': _L1_gnn_in['b_ih'], 'L1_gnn_w_hh': _L1_gnn_in['w_hh'], 'L1_gnn_b_hh': _L1_gnn_in['b_hh'], 'L2_gnn_Wl': _L2_gnn_in['Wl'], 'L2_gnn_bl': _L2_gnn_in['bl'], 'L2_gnn_Ws': _L2_gnn_in['Ws'], 'L2_gnn_bs': _L2_gnn_in['bs'], 'L2_gnn_Wr': _L2_gnn_in['Wr'], 'L2_gnn_br': _L2_gnn_in['br'], 'L2_gnn_ln_w': _L2_gnn_in['ln_w'], 'L2_gnn_ln_b': _L2_gnn_in['ln_b'], 'L3_gnn_W_t': _L3_gnn_in['W_t'], 'L3_gnn_b_t': _L3_gnn_in['b_t'], 'L3_gnn_W_h': _L3_gnn_in['W_h'], 'L3_gnn_theta': _L3_gnn_in['theta']}

def reference(x, adj, L0_gnn_W, L0_gnn_b, L1_gnn_w_se, L1_gnn_b_se, L1_gnn_conv1_w, L1_gnn_bn1_g, L1_gnn_bn1_b, L1_gnn_bn1_m, L1_gnn_bn1_v, L1_gnn_conv2_w, L1_gnn_bn2_g, L1_gnn_bn2_b, L1_gnn_bn2_m, L1_gnn_bn2_v, L1_gnn_w_msg, L1_gnn_b_msg, L1_gnn_w_ih, L1_gnn_b_ih, L1_gnn_w_hh, L1_gnn_b_hh, L2_gnn_Wl, L2_gnn_bl, L2_gnn_Ws, L2_gnn_bs, L2_gnn_Wr, L2_gnn_br, L2_gnn_ln_w, L2_gnn_ln_b, L3_gnn_W_t, L3_gnn_b_t, L3_gnn_W_h, L3_gnn_theta):
    import jax
    import jax.numpy as jnp

    def _L0_gnn_ref(x, adj, W, b):
        import jax, jax.numpy as jnp
        import numpy as np
        B, N, F_IN, F_OUT = (8, 1024, 128, 128)
        n = adj.shape[-1]
        adj = adj + jnp.eye(n, dtype=adj.dtype)[None, :, :]
        deg = adj.sum(axis=-1)
        deg_inv_sqrt = deg ** (-0.5)
        deg_inv_sqrt = jnp.where(jnp.isinf(deg_inv_sqrt), 0.0, deg_inv_sqrt)
        adj_norm = deg_inv_sqrt[:, :, None] * adj * deg_inv_sqrt[:, None, :]
        h = jnp.einsum('bnf,fo->bno', x, W)
        out = jnp.einsum('bnm,bmo->bno', adj_norm, h)
        return out + b

    def _L1_gnn_ref(x, mask, w_se, b_se, conv1_w, bn1_g, bn1_b, bn1_m, bn1_v, conv2_w, bn2_g, bn2_b, bn2_m, bn2_v, w_msg, b_msg, w_ih, b_ih, w_hh, b_hh):
        import jax, jax.numpy as jnp
        import numpy as np
        from jax import lax
        DIM = 128
        EPS = 1e-05

        def _bn(h, g, b, m, v):
            scale = g / jnp.sqrt(v + EPS)
            return h * scale[None, :, None] + (b - m * scale)[None, :, None]

        def _conv1d(h, w, pad):
            return lax.conv_general_dilated(h, w, window_strides=(1,), padding=[(pad, pad)], dimension_numbers=('NCH', 'OIH', 'NCH'))
        d = x.shape[-1]
        xc = jnp.transpose(x, (0, 2, 1))
        h = _bn(_conv1d(xc, conv1_w, 0), bn1_g, bn1_b, bn1_m, bn1_v)
        h = jax.nn.relu(h)
        h = _bn(_conv1d(h, conv2_w, 8), bn2_g, bn2_b, bn2_m, bn2_v)
        x_conv = jnp.transpose(jax.nn.relu(h + xc), (0, 2, 1))
        s = x @ w_se.T + b_se
        sq = jnp.sum(s * s, axis=-1)
        dist = sq[:, :, None] + sq[:, None, :] - 2.0 * jnp.einsum('bnd,bmd->bnm', s, s)
        A = jnp.exp(-dist) * mask
        msg = jax.nn.relu(x @ w_msg.T + b_msg)
        x_nmp = jnp.einsum('bnm,bmd->bnd', A, msg)
        x_in = jnp.concatenate([x_conv, x_nmp], axis=-1)
        gi = x_in @ w_ih.T + b_ih
        gh = x @ w_hh.T + b_hh
        gi_r, gi_z, gi_n = (gi[..., :d], gi[..., d:2 * d], gi[..., 2 * d:])
        gh_r, gh_z, gh_n = (gh[..., :d], gh[..., d:2 * d], gh[..., 2 * d:])
        r = jax.nn.sigmoid(gi_r + gh_r)
        z = jax.nn.sigmoid(gi_z + gh_z)
        nn_ = jnp.tanh(gi_n + r * gh_n)
        return (1.0 - z) * nn_ + z * x

    def _L2_gnn_ref(hidden_state, adjacency_matrix, Wl, bl, Ws, bs, Wr, br, ln_w, ln_b):
        import jax, jax.numpy as jnp
        import numpy as np
        H = 128
        EPS_RENORM = 1e-10
        EPS_LN = 1e-12
        B, N, Hd = hidden_state.shape
        temper = Hd ** 0.5
        u = jnp.einsum('bnh,bmh->bnm', hidden_state, hidden_state) / temper
        scores = jax.nn.softmax(u, axis=-1)
        delta = scores * adjacency_matrix
        att = delta / (jnp.sum(delta, axis=2, keepdims=True) + EPS_RENORM)
        i = jnp.arange(N)[:, None]
        j = jnp.arange(N)[None, :]
        att_left = jnp.where(j > i, att, 0.0)
        att_self = jnp.where(j == i, att, 0.0)
        att_right = jnp.where(j < i, att, 0.0)
        h_left = hidden_state @ Wl.T + bl
        h_self = hidden_state @ Ws.T + bs
        h_right = hidden_state @ Wr.T + br
        ctx = jnp.einsum('bnm,bmh->bnh', att_left, h_left) + jnp.einsum('bnm,bmh->bnh', att_self, h_self) + jnp.einsum('bnm,bmh->bnh', att_right, h_right)
        mu = jnp.mean(ctx, axis=-1, keepdims=True)
        var = jnp.mean((ctx - mu) ** 2, axis=-1, keepdims=True)
        o = ln_w * ((ctx - mu) / jnp.sqrt(var + EPS_LN)) + ln_b
        return jax.nn.relu(o)

    def _L3_gnn_ref(x, adj, W_t, b_t, W_h, theta):
        import jax, jax.numpy as jnp
        import numpy as np
        B, N, D = (4, 2048, 128)
        DENSITY = 0.02
        in_degrees = jnp.sum(adj, axis=-1)
        norm = jnp.power(in_degrees + 1e-06, -0.5)[..., None]
        f_hom = jnp.einsum('bnd,de->bne', x, theta) * norm
        f_hom = jnp.einsum('bnm,bmd->bnd', adj, f_hom) * norm
        f_het = jnp.einsum('bnd,de->bne', x, W_h)
        gate = jax.nn.sigmoid(jnp.einsum('bnd,de->bne', x, W_t) + b_t)
        out = gate * f_hom + (1.0 - gate) * f_het
        return jax.nn.elu(out)
    h = jnp.maximum(_layernorm(x, axis=-1), 0.0)
    x = x + _L0_gnn_ref(h, adj, L0_gnn_W, L0_gnn_b)
    h = jnp.maximum(_layernorm(x, axis=-1), 0.0)
    x = x + _L1_gnn_ref(h, adj, L1_gnn_w_se, L1_gnn_b_se, L1_gnn_conv1_w, L1_gnn_bn1_g, L1_gnn_bn1_b, L1_gnn_bn1_m, L1_gnn_bn1_v, L1_gnn_conv2_w, L1_gnn_bn2_g, L1_gnn_bn2_b, L1_gnn_bn2_m, L1_gnn_bn2_v, L1_gnn_w_msg, L1_gnn_b_msg, L1_gnn_w_ih, L1_gnn_b_ih, L1_gnn_w_hh, L1_gnn_b_hh)
    h = jnp.maximum(_layernorm(x, axis=-1), 0.0)
    x = x + _L2_gnn_ref(h, adj, L2_gnn_Wl, L2_gnn_bl, L2_gnn_Ws, L2_gnn_bs, L2_gnn_Wr, L2_gnn_br, L2_gnn_ln_w, L2_gnn_ln_b)
    h = jnp.maximum(_layernorm(x, axis=-1), 0.0)
    x = x + _L3_gnn_ref(h, adj, L3_gnn_W_t, L3_gnn_b_t, L3_gnn_W_h, L3_gnn_theta)
    return x

_drawn_inputs = setup_inputs


def setup_inputs(seed=0):
    import zlib

    import numpy as np

    out = dict(_drawn_inputs(seed))
    spreads = {'L1_gnn_b_se': (0.0, 2.0),
     'L1_gnn_bn1_g': (1.0, 0.6),
     'L1_gnn_bn1_b': (0.0, 0.463),
     'L1_gnn_bn1_m': (0.0, 0.449),
     'L1_gnn_bn1_v': (1.0, 0.6),
     'L1_gnn_bn2_g': (1.0, 0.6),
     'L1_gnn_bn2_b': (0.0, 0.8),
     'L1_gnn_bn2_m': (0.0, 0.735),
     'L1_gnn_bn2_v': (1.0, 0.6),
     'L1_gnn_b_msg': (0.0, 1.15),
     'L1_gnn_b_ih': (0.0, 0.359),
     'L1_gnn_b_hh': (0.0, 0.552),
     'L2_gnn_ln_w': (1.0, 0.2),
     'L2_gnn_ln_b': (0.0, 0.1)}
    factors = {'L1_gnn_w_se': 198.776,
     'L2_gnn_bl': 4.406,
     'L2_gnn_br': 4.187,
     'L3_gnn_W_t': 8.0,
     'L3_gnn_b_t': 64.0,
     'L1_gnn_w_msg': 3.132}
    for name, (base, spread) in spreads.items():
        noise = np.random.default_rng([zlib.crc32(name.encode()), seed]).standard_normal(out[name].shape)
        drawn = base * np.exp(spread * noise) if base else spread * noise
        out[name] = jnp.asarray(drawn.astype(out[name].dtype))
    for name, factor in factors.items():
        out[name] = (out[name] * factor).astype(out[name].dtype)
    return out
```

```python
from collections import namedtuple
from contextlib import ExitStack

import numpy as np

import concourse.bass as bass
from concourse import mybir

F32 = mybir.dt.float32
F32R = mybir.dt.float32r
ALU = mybir.AluOpType
ACT = mybir.ActivationFunctionType
AX_X = mybir.AxisListType.X

B, N, D = 128, 128, 128
G = 4
GROUPS = B // G
ROUND = 4
TAPS = 17
PAD = TAPS // 2
LN_EPS = 1e-5
L2_LN_EPS = 1e-12
L2_RENORM_EPS = 1e-10
L3_DEG_EPS = 1e-6
BN_EPS = 1e-5

ROWS = ("L0_gnn_b", "L1_gnn_b_msg", "L1_gnn_b_se", "L2_gnn_bl", "L2_gnn_bs", "L2_gnn_br",
        "L2_gnn_ln_w", "L2_gnn_ln_b", "L3_gnn_b_t")
ROW_SIZE = {"L1_gnn_b_se": 3}
ROW_AT = {}
_at = 0
for _name in ROWS:
    ROW_AT[_name] = _at
    _at += ROW_SIZE.get(_name, D)
ROW_TOTAL = _at
COLS = ("bn1_g", "bn1_b", "bn1_m", "bn1_v", "bn2_g", "bn2_b", "bn2_m", "bn2_v",
        "bih_r", "bih_z", "bih_n", "bhh_r", "bhh_z", "bhh_n")
COL_AT = {n: i for i, n in enumerate(COLS)}

class Group(namedtuple("Group", "n slot turn")):
    def has(self, back):
        return not isinstance(self.n, int) or self.n >= back


def group(turn, step, lag):
    s = step - lag
    if isinstance(turn, int) and not 0 <= turn * ROUND + s < GROUPS:
        return None
    return Group(turn * ROUND + s, s % ROUND, turn + s // ROUND)


def build(nc, x, adj, eye, rows, cols, w0, conv1T, conv2T, wmsgT, wihT, whhT, wlsrT, whet, theta, out):
    ctx = ExitStack()

    def sb(name, shape, dt=F32):
        return ctx.enter_context(nc.sbuf_tensor(name, [128, *shape], dt))

    def sem(name):
        return ctx.enter_context(nc.semaphore(name))

    with ctx:
        PS = ctx.enter_context(nc.psum_tensor("banks", [128, 8, 512], F32))

        def bank(b, n=1):
            return PS[:, b:b + n, :].rearrange("p b (g n) -> p (b g) n", n=N)

        def pair_wide(b, w):
            return PS[:, b:b + 2, :].rearrange("p b (g n) -> p (b g) n", n=256)[:, :, 0:w]

        CONV, Q, S1, T6, T7 = 0, 1, 5, 6, 7

        EYE = sb("EYE", [3, N])
        ROWV = sb("ROWV", [ROW_TOTAL])
        COLV = sb("COLV", [len(COLS)])
        CW = sb("CW", [8])
        CG = sb("CG", [4])
        CT = sb("CT", [8])
        W0 = sb("W0", [D])
        WMSG = sb("WMSG", [D + 3])
        WHET = sb("WHET", [2 * D])
        THETA = sb("THETA", [D])
        NSPLIT = TAPS * D + D + 2 * 3 * D + 3 * D + 3 * D
        WF = sb("WF", [3 * D])
        WHI = sb("WHI", [NSPLIT], F32R)
        WLO = sb("WLO", [NSPLIT], F32R)
        MHALF = sb("MHALF", [12])
        EPS = sb("EPS", [8])
        at = 0
        where = {}
        for name, size in (("conv2", TAPS * D), ("conv1", D), ("wih", 6 * D), ("whh", 3 * D), ("wlsr", 3 * D)):
            where[name] = at
            at += size

        def w(name, c, n=1):
            a = where[name] + c * D
            return WHI[:, a:a + n * D], WLO[:, a:a + n * D]

        X = sb("X", [4, G, D])
        ADJ = sb("ADJ", [2, G, N])
        ADJT = sb("ADJT", [4, G, N])
        ADJI = sb("ADJI", [G, N])
        XB = sb("XB", [G, D])
        DEG = sb("DEG", [4, G])
        ST = [sb(f"ST{k}", [G, 6]) for k in range(5)]
        MV = [sb(f"MV{k}", [2, G, 2]) for k in range(5)]
        NM = [sb(f"NM{k}", [2, G]) for k in range(5)]
        VE = [sb(f"VE{k}", [2, G]) for k in range(5)]
        RS = [sb(f"RS{k}", [2, G]) for k in range(5)]
        NR = [sb(f"NR{k}", [2, G]) for k in range(5)]
        PW = sb("PW", [12])
        ZD = sb("ZD", [G])
        KEEP = sb("KEEP", [G])
        DN = sb("DN", [4, 12])
        XH0 = sb("XH0", [G, D])
        HP = sb("HP", [G, D])
        UT = sb("UT", [G, N])
        X1 = sb("X1", [4, G, D])
        XH1 = sb("XH1", [G, D])
        H1T = sb("H1T", [4, G, N])
        H1H = sb("H1H", [4, G, N], F32R)
        H1L = sb("H1L", [4, G, N], F32R)
        C1 = sb("C1", [G, N])
        C1H = sb("C1H", [G, N + 2 * PAD], F32R)
        C1L = sb("C1L", [G, N + 2 * PAD], F32R)
        MSG = sb("MSG", [G, D])
        SS = sb("SS", [G, 3])
        SLR = sb("SLR", [G, 2, 8])
        LRT = ctx.enter_context(nc.sbuf_tensor("LRT", [8, 2, G, N], F32))
        EA = sb("EA", [G, N])
        AT = sb("AT", [G, N])
        NMH = sb("NMH", [2, G, N], F32R)
        NML = sb("NML", [2, G, N], F32R)
        XCP = sb("XCP", [G, N])
        XCH = sb("XCH", [G, N], F32R)
        XCL = sb("XCL", [G, N], F32R)
        TR = sb("TR", [G, N])
        TZ = sb("TZ", [G, N])
        Q2 = sb("Q2", [G, N])
        DH = sb("DH", [G, N])
        X2 = sb("X2", [2, G, D])
        XH2 = sb("XH2", [G, D])
        H2T = sb("H2T", [G, N])
        H2H = sb("H2H", [G, N], F32R)
        H2L = sb("H2L", [G, N], F32R)
        EE = sb("EE", [G, N])
        DE = sb("DE", [G, N])
        DL = sb("DL", [G, N])
        DR = sb("DR", [G, N])
        DI = sb("DI", [G, N])
        ZS = sb("ZS", [2, G])
        DG = sb("DG", [2, G])
        HLR = sb("HLR", [G, 3, D + 4])
        HSD = sb("HSD", [G, D])
        CC = sb("CC", [G, D])
        DEN = sb("DEN", [2, 2, G])
        CH = sb("CH", [G, D])
        X3 = sb("X3", [2, G, D])
        XH3 = sb("XH3", [G, D])
        HN = sb("HN", [G, D])
        H3T = sb("H3T", [G, N])
        G3T = sb("G3T", [G, N])
        HET = sb("HET", [G, D])
        FH = sb("FH", [G, D])
        GP = sb("GP", [G, D])
        MN = sb("MN", [G, D])
        OUT = sb("OUT", [2, G, D])

        x_in = [sem(f"x_in{s}") for s in range(4)]
        adj_in = [sem(f"adj_in{s}") for s in range(4)]
        out_stored = [sem(f"out_stored{s}") for s in range(4)]
        consts_in = sem("consts_in")
        weights_in = sem("weights_in")
        pieces_in = [sem(f"piece_in{k}") for k in range(5)]
        piece_hi = sem("piece_hi")
        piece_lo = sem("piece_lo")
        consts_pool = sem("consts_pool")
        consts_ready = sem("consts_ready")
        (pe_conv1, pe_msg, pe_hn, pe_r, pe_z, pe_in, pe_adjT, pe_h3T, pe_g3, pe_sT, pe_u0, pe_hg,
         pe_fhom, pe_dist, pe_y0, pe_gruT, pe_nmp, pe_h2T, pe_h1T, pe_sim, pe_hlsr, pe_conv2,
         pe_ctx) = [sem("pe_" + s) for s in
                    "conv1 msg hn r z in adjT h3T g3 sT u0 hg fhom dist y0 gruT nmp h2T h1T sim hlsr conv2 ctx".split()]
        (a_adjT, a_u0, a_xh1, a_h1T, a_h1H, a_c1, a_c1H, a_msg, a_sT, a_exp, a_nmH, a_xcH, a_r, a_q2,
         a_z, a_nn, a_xh2, a_h2T, a_h2H, a_sim, a_ch, a_h3T, a_g3, a_het, a_gate, a_ex) = [
            sem("a_" + s) for s in
            "adjT u0 xh1 h1T h1H c1 c1H msg sT exp nmH xcH r q2 z nn xh2 h2T h2H sim ch h3T g3 het gate ex".split()]
        (v_deg, v_xh0, v_hp, v_t1, v_x1, v_h1L, v_c1L, v_msgp, v_s, v_s2, v_slr, v_nmL, v_xcp,
         v_xcf, v_xcL, v_rq, v_ni, v_dh, v_ez, v_gt, v_x2, v_hlsr, v_de, v_z, v_diag, v_cc, v_den0, v_den,
         v_x3, v_xh3, v_hn, v_fh, v_gp, v_dd, v_e2, v_v1, v_mn, v_el, v_out) = [
            sem("v_" + s) for s in
            ("deg xh0 hp t1 x1 h1L c1L msgp s s2 slr nmL xcp xcf xcL rq ni dh ez gt x2 hlsr de z "
             "diag cc den0 den x3 xh3 hn fh gp dd e2 v1 mn el out").split()]
        v_st = [sem(f"v_st{k}") for k in range(5)]
        v_nm = [sem(f"v_nm{k}") for k in range(5)]
        v_mv = [sem(f"v_mv{k}") for k in range(5)]
        p_rs = [sem(f"p_rs{k}") for k in range(5)]
        (p_adji, p_xb, p_at, p_dl, p_di, p_hsd, p_lnb, p_h2L) = [
            sem("p_" + s) for s in "adji xb at dl di hsd lnb h2L".split()]
        v_deg0 = sem("v_deg0")
        v_zd = sem("v_zd")

        def row(name):
            n = ROW_SIZE.get(name, D)
            return ROWV[:, ROW_AT[name]:ROW_AT[name] + n].unsqueeze(1).to_broadcast([128, G, n])

        def per_graph(v):
            return v.unsqueeze(2).to_broadcast([128, G, D])

        def mask(k):
            return EYE[:, k, :].unsqueeze(1).to_broadcast([128, G, N])

        def flat(t):
            return t.rearrange("p g n -> p (g n)")

        ident = EYE[:, 0, :]
        x_d = x.rearrange("(s g) n d -> s n g d", g=G)
        adj_d = adj.rearrange("(s g) n m -> s n g m", g=G)
        out_d = out.rearrange("(s g) n d -> s n g d", g=G)

        def schedule(engine, one_step):
            for step in range(ROUND):
                one_step(0, step)
            with engine.Fori(1, GROUPS // ROUND) as turn:
                for step in range(ROUND):
                    one_step(turn, step)
            for step in range(3):
                one_step(GROUPS // ROUND, step)

        pieces = (("conv1", conv1T, 1), ("wih", wihT, 6), ("whh", whhT, 3), ("wlsr", wlsrT, 3),
                  ("conv2", conv2T, TAPS))
        PIECE = 3
        cuts = [(name, src, c, min(PIECE, n - c)) for name, src, n in pieces for c in range(0, n, PIECE)]
        block = ctx.enter_context(nc.Block())

        @block.sync
        def _(sp):
            sp.dma_start(EYE[:], eye).then_inc(consts_in, 16)
            sp.dma_start(COLV[:], cols).then_inc(consts_in, 16)
            sp.dma_start(ROWV[:], rows.partition_broadcast(128)).then_inc(consts_in, 16)

            def load(g):
                if g.has(4):
                    sp.wait_ge(p_xb, g.n - 3)
                if g.has(4):
                    sp.wait_ge(v_xh0, g.n - 3)
                sp.dma_start(X[:, g.slot], x_d[g.n]).then_inc(x_in[g.slot], 16)
                if g.has(2):
                    sp.wait_ge(pe_adjT, g.n - 1)
                if g.has(2):
                    sp.wait_ge(v_deg, g.n - 1)
                sp.dma_start(ADJ[:, g.slot % 2], adj_d[g.n]).then_inc(adj_in[g.slot], 16)

            def store(g):
                sp.wait_ge(v_out, g.n + 1)
                sp.dma_start(out_d[g.n], OUT[:, g.slot % 2]).then_inc(out_stored[g.slot], 16)

            def weights():
                sp.dma_start(W0[:], w0).then_inc(weights_in, 16)
                sp.dma_start(WMSG[:], wmsgT).then_inc(weights_in, 16)
                sp.dma_start(WHET[:], whet).then_inc(weights_in, 16)
                sp.dma_start(THETA[:], theta).then_inc(weights_in, 16)
                for k, (name, src, c, n) in enumerate(cuts):
                    if k:
                        sp.wait_ge(piece_lo, k)
                    sp.dma_start(WF[:, 0:n * D], src[:, c * D:(c + n) * D]).then_inc(pieces_in[0], 16)

            def one_step(turn, step):
                g, d = group(turn, step, -1), group(turn, step, 3)
                if isinstance(turn, int) and turn == 0 and step == 0:
                    load(group(0, 0, 0))
                    load(group(0, 1, 0))
                    weights()
                elif g is not None and (not isinstance(turn, int) or turn * ROUND + step + 1 < GROUPS):
                    load(g)
                if d is not None:
                    store(d)

            for step in range(ROUND):
                one_step(0, step)
            with sp.Fori(1, GROUPS // ROUND - 1) as turn:
                for step in range(ROUND):
                    one_step(turn, step)
            for step in range(ROUND):
                one_step(GROUPS // ROUND - 1, step)
            for step in range(3):
                one_step(GROUPS // ROUND, step)
            for s in range(4):
                sp.wait_ge(out_stored[s], 16 * (GROUPS // 4))

        @block.gpsimd
        def _(pool):
            links = [0]

            def small(ins):
                links[0] += 1
                ins.then_inc(consts_pool, 1)
                pool.wait_ge(consts_pool, links[0])

            def col(n):
                return COLV[:, COL_AT[n]:COL_AT[n] + 1]

            small(nc.gpsimd.memset(MHALF[:], -0.5))
            small(nc.gpsimd.memset(EPS[:, 0:4], LN_EPS))
            small(nc.gpsimd.memset(EPS[:, 4:8], L2_LN_EPS))
            small(nc.gpsimd.memset(HLR[:], 1.0))
            small(nc.gpsimd.memset(SLR[:], 1.0))
            small(nc.gpsimd.memset(C1H[:].bitcast(F32), 0.0))
            small(nc.gpsimd.memset(C1L[:].bitcast(F32), 0.0))
            pool.wait_ge(consts_in, 48)
            for k in (0, 1):
                bn = f"bn{k + 1}_"
                small(nc.gpsimd.tensor_scalar(CT[:, 0:1], col(bn + "v"), BN_EPS, None, ALU.add))
                small(nc.gpsimd.tensor_tensor(CT[:, 1:2], CT[:, 0:1], MHALF[:, 0:1], ALU.pow))
                small(nc.gpsimd.tensor_tensor(CW[:, 2 * k:2 * k + 1], CT[:, 1:2], col(bn + "g"), ALU.mult))
                small(nc.gpsimd.tensor_tensor(CT[:, 2:3], CW[:, 2 * k:2 * k + 1], col(bn + "m"), ALU.mult))
                small(nc.gpsimd.tensor_tensor(CW[:, 2 * k + 1:2 * k + 2], col(bn + "b"), CT[:, 2:3], ALU.subtract))
            for k, gate in enumerate("rz"):
                small(nc.gpsimd.tensor_tensor(CT[:, 3:4], col("bih_" + gate), col("bhh_" + gate), ALU.add))
                small(nc.gpsimd.tensor_scalar(CG[:, k:k + 1], CT[:, 3:4], 0.5, None, ALU.mult))
            small(nc.gpsimd.tensor_scalar(CG[:, 2:3], col("bhh_n"), 0.5, None, ALU.mult))
            nc.gpsimd.tensor_copy(CG[:, 3:4], col("bih_n")).then_inc(consts_ready, 1)

            p_pw0 = sem("p_pw0")
            p_dn0 = sem("p_dn0")

            def stats0(g):
                pool.wait_ge(v_mv[0], g.n + 1)
                pool.wait_ge(v_deg, g.n + 1)
                s, p = g.slot, g.slot % 2
                nc.gpsimd.tensor_tensor(PW[:, 0:4], MV[0][:, p, :, 1], EPS[:, 0:4], ALU.add).then_inc(p_pw0, 1)
                pool.wait_ge(p_pw0, g.n + 1)
                nc.gpsimd.tensor_tensor(DN[:, s], PW[:], MHALF[:], ALU.pow).then_inc(p_dn0, 1)
                pool.wait_ge(p_dn0, g.n + 1)
                nc.gpsimd.tensor_tensor(DN[:, s, 4:8], DN[:, s, 4:8], KEEP[:], ALU.mult).then_inc(p_rs[0], 1)

            p_ve = [sem(f"p_ve{k}") for k in range(1, 5)]
            p_pw = [sem(f"p_pw{k}") for k in range(1, 5)]

            def rstd(k, g):
                p = g.slot % 2
                pool.wait_ge(v_mv[k], g.n + 1)
                nc.gpsimd.tensor_tensor(VE[k][:, p], MV[k][:, p, :, 1], EPS[:, 0:4], ALU.add).then_inc(p_ve[k - 1], 1)
                pool.wait_ge(p_ve[k - 1], g.n + 1)
                nc.gpsimd.tensor_tensor(RS[k][:, p], VE[k][:, p], MHALF[:, 0:4], ALU.pow).then_inc(p_pw[k - 1], 1)
                pool.wait_ge(p_pw[k - 1], g.n + 1)
                nc.gpsimd.tensor_tensor(NR[k][:, p], NM[k][:, p], RS[k][:, p], ALU.mult).then_inc(p_rs[k], 1)

            p_d2 = sem("p_d2")
            p_d3 = sem("p_d3")

            def rstd_ctx(g):
                p = g.slot % 2
                pool.wait_ge(v_den, g.n + 1)
                nc.gpsimd.tensor_tensor(DEN[:, 0, p], DEN[:, 1, p], DEN[:, 1, p], ALU.mult).then_inc(p_d2, 1)
                pool.wait_ge(p_d2, g.n + 1)
                nc.gpsimd.tensor_tensor(VE[4][:, p], DEN[:, 0, p], EPS[:, 4:8], ALU.mult).then_inc(p_d3, 1)
                pool.wait_ge(p_d3, g.n + 1)
                pool.wait_ge(v_mv[4], g.n + 1)
                nc.gpsimd.tensor_tensor(DEN[:, 0, p], VE[4][:, p], MV[4][:, p, :, 1], ALU.add).then_inc(p_ve[3], 1)
                pool.wait_ge(p_ve[3], g.n + 1)
                nc.gpsimd.tensor_tensor(RS[4][:, p], DEN[:, 0, p], MHALF[:, 0:4], ALU.pow).then_inc(p_pw[3], 1)
                pool.wait_ge(p_pw[3], g.n + 1)
                nc.gpsimd.tensor_tensor(NR[4][:, p], NM[4][:, p], RS[4][:, p], ALU.mult).then_inc(p_rs[4], 1)

            def adj_plus_eye(g):
                pool.wait_ge(a_adjT, g.n + 1)
                if g.has(1):
                    pool.wait_ge(pe_u0, g.n)
                nc.gpsimd.tensor_tensor(ADJI[:], ADJT[:, g.slot], mask(0), ALU.add).then_inc(p_adji, 1)

            def x_plus_bias(g):
                pool.wait_ge(x_in[g.slot], (g.turn + 1) * 16)
                if g.has(1):
                    pool.wait_ge(v_x1, g.n)
                nc.gpsimd.tensor_tensor(XB[:], X[:, g.slot], row("L0_gnn_b"), ALU.add).then_inc(p_xb, 1)

            def gauss_mask(g):
                pool.wait_ge(a_exp, g.n + 1)
                if g.has(1):
                    pool.wait_ge(pe_nmp, g.n)
                nc.gpsimd.tensor_tensor(AT[:], EA[:], ADJT[:, g.slot], ALU.mult).then_inc(p_at, 1)

            def h2_low(g):
                pool.wait_ge(a_h2T, g.n + 1)
                pool.wait_ge(a_h2H, g.n + 1)
                if g.has(1):
                    pool.wait_ge(pe_hlsr, g.n)
                nc.gpsimd.tensor_tensor(H2L[:], H2T[:], H2H[:].bitcast(F32), ALU.subtract).then_inc(p_h2L, 1)

            def triangles(g):
                pool.wait_ge(v_de, g.n + 1)
                if g.has(1):
                    pool.wait_ge(pe_ctx, g.n)
                nc.gpsimd.tensor_tensor(DL[:], DE[:], mask(1), ALU.mult)
                nc.gpsimd.tensor_tensor(DR[:], DE[:], mask(2), ALU.mult).then_inc(p_dl, 1)
                if g.has(1):
                    pool.wait_ge(v_diag, g.n)
                nc.gpsimd.tensor_tensor(DI[:], DE[:], mask(0), ALU.mult).then_inc(p_di, 1)

            def self_part(g):
                pool.wait_ge(v_diag, g.n + 1)
                pool.wait_ge(v_hlsr, g.n + 1)
                if g.has(1):
                    pool.wait_ge(v_cc, g.n)
                nc.gpsimd.tensor_tensor(HSD[:], HLR[:, :, 1, 0:D], per_graph(DG[:, g.slot % 2]),
                                        ALU.mult).then_inc(p_hsd, 1)

            p_lnw = sem("p_lnw")

            def ln_affine(g):
                pool.wait_ge(a_ch, g.n + 1)
                nc.gpsimd.tensor_tensor(CH[:], CH[:], row("L2_gnn_ln_w"), ALU.mult).then_inc(p_lnw, 1)
                pool.wait_ge(p_lnw, g.n + 1)
                if g.has(1):
                    pool.wait_ge(v_x3, g.n)
                nc.gpsimd.tensor_tensor(CH[:], CH[:], row("L2_gnn_ln_b"), ALU.add).then_inc(p_lnb, 1)

            def one_step(turn, step):
                a, b, c, d = (group(turn, step, lag) for lag in range(4))
                if d:
                    rstd_ctx(d)
                if a:
                    stats0(a)
                    x_plus_bias(a)
                if d:
                    ln_affine(d)
                if a:
                    adj_plus_eye(a)
                if d:
                    rstd(3, d)
                if b:
                    gauss_mask(b)
                if a:
                    rstd(1, a)
                if c:
                    rstd(2, c)
                if c:
                    h2_low(c)
                    triangles(c)
                    self_part(c)

            schedule(pool, one_step)

        @block.scalar
        def _(act):
            act.wait_ge(consts_ready, 1)

            def adj_t(g):
                act.wait_ge(pe_adjT, g.n + 1)
                if g.has(4):
                    act.wait_ge(pe_g3, g.n - 3)
                nc.scalar.activation(ADJT[:, g.slot], bank(S1), ACT.Copy).then_inc(a_adjT, 1)

            def agg0(g):
                act.wait_ge(pe_u0, g.n + 1)
                nc.scalar.activation(UT[:], bank(S1), ACT.Copy).then_inc(a_u0, 1)

            def norm(k, g, dst, src, semaphore, func):
                p = g.slot % 2
                act.wait_ge(p_rs[k], g.n + 1)
                for j in range(G):
                    last = nc.scalar.activation(dst[:, j], src[:, j], func, scale=RS[k][:, p, j:j + 1],
                                                bias=NR[k][:, p, j:j + 1])
                last.then_inc(semaphore, 1)

            def h1(g):
                act.wait_ge(pe_h1T, g.n + 1)
                nc.scalar.activation(H1T[:, g.slot], bank(S1), ACT.Copy).then_inc(a_h1T, 1)
                nc.scalar.activation(H1H[:, g.slot], bank(S1), ACT.Copy).then_inc(a_h1H, 1)

            def conv1(g):
                act.wait_ge(pe_conv1, g.n + 1)
                if g.has(1):
                    act.wait_ge(v_c1L, g.n)
                nc.scalar.activation(C1[:], bank(S1), ACT.Relu, scale=CW[:, 0:1], bias=CW[:, 1:2]).then_inc(a_c1, 1)
                act.wait_ge(a_c1, g.n + 1)
                nc.scalar.activation(C1H[:, :, PAD:PAD + N], C1[:], ACT.Copy).then_inc(a_c1H, 1)

            def message(g):
                act.wait_ge(v_msgp, g.n + 1)
                nc.scalar.activation(MSG[:], MSG[:], ACT.Relu).then_inc(a_msg, 1)

            def s_t(g):
                act.wait_ge(pe_sT, g.n + 1)
                nc.scalar.activation(LRT[0:5].rearrange("p l g n -> p l (g n)"), PS[0:5, T6:T7 + 1, :],
                                     ACT.Copy).then_inc(a_sT, 1)

            def gauss(g):
                act.wait_ge(pe_dist, g.n + 1)
                if g.has(1):
                    act.wait_ge(p_at, g.n)
                nc.scalar.activation(EA[:], bank(T6), ACT.Exp).then_inc(a_exp, 1)

            def nmp(g):
                act.wait_ge(pe_nmp, g.n + 1)
                nc.scalar.activation(NMH[:, g.slot % 2], bank(T6), ACT.Copy).then_inc(a_nmH, 1)

            def x_conv(g):
                act.wait_ge(v_xcf, g.n + 1)
                nc.scalar.activation(XCH[:], XCP[:], ACT.Copy).then_inc(a_xcH, 1)

            def gates(g):
                act.wait_ge(pe_hn, g.n + 1)
                nc.scalar.activation(Q2[:], bank(Q + 2), ACT.Identity, scale=0.5, bias=CG[:, 2:3]).then_inc(a_q2, 1)
                act.wait_ge(pe_r, g.n + 1)
                nc.scalar.activation(TR[:], bank(Q), ACT.Tanh, scale=0.5, bias=CG[:, 0:1]).then_inc(a_r, 1)
                act.wait_ge(pe_z, g.n + 1)
                nc.scalar.activation(TZ[:], bank(Q + 1), ACT.Tanh, scale=0.5, bias=CG[:, 1:2]).then_inc(a_z, 1)

            def candidate(g):
                act.wait_ge(v_ni, g.n + 1)
                nc.scalar.activation(Q2[:], Q2[:], ACT.Tanh, bias=CG[:, 3:4]).then_inc(a_nn, 1)

            def h2(g):
                act.wait_ge(pe_h2T, g.n + 1)
                nc.scalar.activation(H2T[:], bank(T7), ACT.Copy).then_inc(a_h2T, 1)
                nc.scalar.activation(H2H[:], bank(T7), ACT.Copy).then_inc(a_h2H, 1)

            def similarity(g):
                act.wait_ge(pe_sim, g.n + 1)
                if g.has(1):
                    act.wait_ge(v_z, g.n)
                nc.scalar.activation(EE[:], bank(T7), ACT.Exp, scale=float(D) ** -0.5).then_inc(a_sim, 1)

            def h3(g):
                act.wait_ge(pe_h3T, g.n + 1)
                nc.scalar.activation(H3T[:], bank(Q), ACT.Relu).then_inc(a_h3T, 1)
                act.wait_ge(pe_g3, g.n + 1)
                nc.scalar.activation(G3T[:], bank(Q + 1), ACT.Copy).then_inc(a_g3, 1)

            def het(g):
                act.wait_ge(pe_hg, g.n + 1)
                if g.has(1):
                    act.wait_ge(v_v1, g.n)
                nc.scalar.activation(HET[:], bank(Q), ACT.Copy).then_inc(a_het, 1)

            def gate(g):
                act.wait_ge(v_gp, g.n + 1)
                nc.scalar.activation(GP[:], GP[:], ACT.Tanh, scale=0.5).then_inc(a_gate, 1)

            def elu_exp(g):
                act.wait_ge(v_mn, g.n + 1)
                nc.scalar.activation(MN[:], MN[:], ACT.Exp).then_inc(a_ex, 1)

            def one_step(turn, step):
                a, b, c, d = (group(turn, step, lag) for lag in range(4))
                if c:
                    x_conv(c)
                if b:
                    conv1(b)
                    message(b)
                if d:
                    norm(4, d, CH, CC, a_ch, ACT.Identity)
                if c:
                    gates(c)
                if a:
                    adj_t(a)
                if c:
                    candidate(c)
                if b:
                    s_t(b)
                if a:
                    agg0(a)
                if d:
                    h3(d)
                if b:
                    gauss(b)
                if d:
                    het(d)
                    gate(d)
                if a:
                    norm(1, a, XH1, X1[:, a.slot], a_xh1, ACT.Relu)
                if c:
                    norm(2, c, XH2, X2[:, c.slot % 2], a_xh2, ACT.Relu)
                if d:
                    elu_exp(d)
                if b:
                    nmp(b)
                if c:
                    h2(c)
                if a:
                    h1(a)
                if c:
                    similarity(c)

            schedule(act, one_step)

        @block.vector
        def _(dve):
            vv = nc.vector
            for k, (name, src, c, n) in enumerate(cuts):
                hi, lo = w(name, c, n)
                dve.wait_ge(pieces_in[0], 16 * (k + 1))
                vv.tensor_copy(hi, WF[:, 0:n * D]).then_inc(piece_hi, 1)
                dve.wait_ge(piece_hi, k + 1)
                vv.tensor_tensor(lo, WF[:, 0:n * D], hi.bitcast(F32), ALU.subtract).then_inc(piece_lo, 1)
            dve.wait_ge(consts_ready, 1)

            def bn(k, g, src):
                p = g.slot % 2
                for j in range(G):
                    last = vv.bn_stats(ST[k][:, j], src[:, j])
                last.then_inc(v_st[k], 1)
                dve.wait_ge(v_st[k], g.n + 1)
                vv.tensor_scalar(NM[k][:, p], ST[k][:, :, 1], -0.5, None, ALU.mult).then_inc(v_nm[k], 1)
                for j in range(G):
                    last = vv.bn_aggr(MV[k][:, p, j], ST[k][:, j])
                dve.wait_ge(v_nm[k], g.n + 1)
                vv.scalar_tensor_tensor(NM[k][:, p], ST[k][:, :, 4], -0.5, NM[k][:, p], ALU.mult,
                                        ALU.add).then_inc(v_mv[k], 1)

            def degree(g):
                dve.wait_ge(adj_in[g.slot], (g.turn + 1) * 16)
                deg = DEG[:, g.slot]
                vv.tensor_reduce(deg, ADJ[:, g.slot % 2], AX_X, ALU.add).then_inc(v_deg0, 1)
                dve.wait_ge(v_deg0, g.n + 1)
                if g.has(1):
                    dve.wait_ge(p_rs[0], g.n)
                vv.tensor_scalar(ZD[:], deg, 1.0, 0.0, ALU.add, ALU.is_equal).then_inc(v_zd, 1)
                vv.tensor_scalar(KEEP[:], deg, 1.0, 0.0, ALU.add, ALU.not_equal)
                vv.tensor_scalar(PW[:, 8:12], deg, L3_DEG_EPS, None, ALU.add)
                dve.wait_ge(v_zd, g.n + 1)
                vv.scalar_tensor_tensor(PW[:, 4:8], deg, 1.0, ZD[:], ALU.add, ALU.add).then_inc(v_deg, 1)

            def bn0(g):
                dve.wait_ge(x_in[g.slot], (g.turn + 1) * 16)
                bn(0, g, X[:, g.slot])

            def h0(g):
                s, p = g.slot, g.slot % 2
                dve.wait_ge(p_rs[0], g.n + 1)
                for j in range(G):
                    last = vv.tensor_scalar(XH0[:, j], X[:, s, j], MV[0][:, p, j, 0:1], DN[:, s, j:j + 1],
                                            ALU.subtract, ALU.mult)
                last.then_inc(v_xh0, 1)
                dve.wait_ge(v_xh0, g.n + 1)
                if g.has(1):
                    dve.wait_ge(pe_u0, g.n)
                vv.scalar_tensor_tensor(HP[:], XH0[:], 0.0, per_graph(DN[:, s, 4:8]), ALU.max,
                                        ALU.mult).then_inc(v_hp, 1)

            def x1(g):
                s = g.slot
                dve.wait_ge(pe_y0, g.n + 1)
                vv.tensor_tensor(X1[:, s], bank(S1), per_graph(DN[:, s, 4:8]), ALU.mult).then_inc(v_t1, 1)
                dve.wait_ge(v_t1, g.n + 1)
                dve.wait_ge(p_xb, g.n + 1)
                vv.tensor_tensor(X1[:, s], X1[:, s], XB[:], ALU.add).then_inc(v_x1, 1)
                dve.wait_ge(v_x1, g.n + 1)
                bn(1, g, X1[:, s])

            def h1_low(g):
                dve.wait_ge(a_h1T, g.n + 1)
                dve.wait_ge(a_h1H, g.n + 1)
                vv.tensor_tensor(H1L[:, g.slot], H1T[:, g.slot], H1H[:, g.slot].bitcast(F32),
                                 ALU.subtract).then_inc(v_h1L, 1)

            def c1_low(g):
                dve.wait_ge(a_c1H, g.n + 1)
                vv.tensor_tensor(C1L[:, :, PAD:PAD + N], C1[:], C1H[:, :, PAD:PAD + N].bitcast(F32),
                                 ALU.subtract).then_inc(v_c1L, 1)

            def message(g):
                dve.wait_ge(pe_msg, g.n + 1)
                if g.has(1):
                    dve.wait_ge(pe_nmp, g.n)
                wide = pair_wide(T6, D + 3)
                vv.tensor_tensor(MSG[:], wide[:, :, 0:D], row("L1_gnn_b_msg"), ALU.add).then_inc(v_msgp, 1)
                vv.tensor_tensor(SLR[:, :, 1, 0:3], wide[:, :, D:D + 3], row("L1_gnn_b_se"),
                                 ALU.add).then_inc(v_s, 1)
                dve.wait_ge(v_s, g.n + 1)
                vv.tensor_tensor(SS[:], SLR[:, :, 1, 0:3], SLR[:, :, 1, 0:3], ALU.mult).then_inc(v_s2, 1)
                vv.tensor_scalar(SLR[:, :, 0, 0:3], SLR[:, :, 1, 0:3], 2.0, None, ALU.mult)
                dve.wait_ge(v_s2, g.n + 1)
                vv.tensor_reduce(SLR[:, :, 0, 3:4], SS[:], AX_X, ALU.add, negate=True)
                vv.tensor_reduce(SLR[:, :, 1, 4:5], SS[:], AX_X, ALU.add, negate=True).then_inc(v_slr, 1)

            def nmp_low(g):
                dve.wait_ge(a_nmH, g.n + 1)
                vv.tensor_tensor(NML[:, g.slot % 2], bank(T6), NMH[:, g.slot % 2].bitcast(F32),
                                 ALU.subtract).then_inc(v_nmL, 1)

            def x_conv(g):
                dve.wait_ge(pe_conv2, g.n + 1)
                vv.scalar_tensor_tensor(flat(XCP[:]), flat(bank(CONV)), CW[:, 2:3], flat(H1T[:, g.slot]),
                                        ALU.mult, ALU.add).then_inc(v_xcp, 1)
                dve.wait_ge(v_xcp, g.n + 1)
                if g.has(1):
                    dve.wait_ge(a_xcH, g.n)
                vv.tensor_scalar(XCP[:], XCP[:], CW[:, 3:4], 0.0, ALU.add, ALU.max).then_inc(v_xcf, 1)

            def x_conv_low(g):
                dve.wait_ge(a_xcH, g.n + 1)
                vv.tensor_tensor(XCL[:], XCP[:], XCH[:].bitcast(F32), ALU.subtract).then_inc(v_xcL, 1)

            def new_gate(g):
                dve.wait_ge(a_q2, g.n + 1)
                dve.wait_ge(a_r, g.n + 1)
                vv.scalar_tensor_tensor(Q2[:], TR[:], 1.0, Q2[:], ALU.add, ALU.mult).then_inc(v_rq, 1)
                dve.wait_ge(v_rq, g.n + 1)
                dve.wait_ge(pe_in, g.n + 1)
                vv.tensor_tensor(Q2[:], bank(Q + 3), Q2[:], ALU.add).then_inc(v_ni, 1)

            def blend(g):
                dve.wait_ge(a_nn, g.n + 1)
                vv.tensor_tensor(DH[:], H1T[:, g.slot], Q2[:], ALU.subtract).then_inc(v_dh, 1)
                dve.wait_ge(v_dh, g.n + 1)
                dve.wait_ge(a_z, g.n + 1)
                vv.scalar_tensor_tensor(DH[:], TZ[:], 1.0, DH[:], ALU.add, ALU.mult).then_inc(v_ez, 1)
                dve.wait_ge(v_ez, g.n + 1)
                vv.scalar_tensor_tensor(DH[:], DH[:], 0.5, Q2[:], ALU.mult, ALU.add).then_inc(v_gt, 1)

            def x2(g):
                dve.wait_ge(pe_gruT, g.n + 1)
                vv.tensor_tensor(X2[:, g.slot % 2], bank(T7), X1[:, g.slot], ALU.add).then_inc(v_x2, 1)
                dve.wait_ge(v_x2, g.n + 1)
                bn(2, g, X2[:, g.slot % 2])

            def values(g):
                dve.wait_ge(pe_hlsr, g.n + 1)
                bias = ROWV[:, ROW_AT["L2_gnn_bl"]:ROW_AT["L2_gnn_bl"] + 3 * D].rearrange("p (w n) -> p w n", w=3)
                vv.tensor_tensor(HLR[:, :, :, 0:D],
                                 PS[:, Q:Q + 4, 0:3 * D].rearrange("p g (w n) -> p g w n", w=3),
                                 bias.unsqueeze(1).to_broadcast([128, G, 3, D]), ALU.add).then_inc(v_hlsr, 1)

            def delta(g):
                dve.wait_ge(a_sim, g.n + 1)
                if g.has(1):
                    dve.wait_ge(p_di, g.n)
                vv.tensor_tensor(DE[:], EE[:], ADJT[:, g.slot], ALU.mult).then_inc(v_de, 1)
                vv.tensor_reduce(ZS[:, g.slot % 2], EE[:], AX_X, ALU.add).then_inc(v_z, 1)

            def diagonal(g):
                dve.wait_ge(p_di, g.n + 1)
                vv.tensor_reduce(DG[:, g.slot % 2], DI[:], AX_X, ALU.add).then_inc(v_diag, 1)

            def context(g):
                p = g.slot % 2
                dve.wait_ge(pe_ctx, g.n + 1)
                dve.wait_ge(p_hsd, g.n + 1)
                if g.has(1):
                    dve.wait_ge(a_ch, g.n)
                wide = pair_wide(T6, D + 1)
                vv.tensor_tensor(CC[:], wide[:, :, 0:D], HSD[:], ALU.add).then_inc(v_cc, 1)
                vv.tensor_tensor(DEN[:, 0, p], wide[:, :, D:D + 1].rearrange("p g o -> p (g o)"), DG[:, p],
                                 ALU.add).then_inc(v_den0, 1)
                dve.wait_ge(v_den0, g.n + 1)
                vv.scalar_tensor_tensor(DEN[:, 1, p], ZS[:, p], L2_RENORM_EPS, DEN[:, 0, p], ALU.mult,
                                        ALU.add).then_inc(v_den, 1)
                dve.wait_ge(v_cc, g.n + 1)
                bn(4, g, CC)

            def x3(g):
                dve.wait_ge(p_lnb, g.n + 1)
                vv.scalar_tensor_tensor(X3[:, g.slot % 2], CH[:], 0.0, X2[:, g.slot % 2], ALU.max,
                                        ALU.add).then_inc(v_x3, 1)
                dve.wait_ge(v_x3, g.n + 1)
                bn(3, g, X3[:, g.slot % 2])

            def h3(g):
                p = g.slot % 2
                dve.wait_ge(p_rs[3], g.n + 1)
                for j in range(G):
                    last = vv.tensor_scalar(XH3[:, j], X3[:, p, j], MV[3][:, p, j, 0:1], RS[3][:, p, j:j + 1],
                                            ALU.subtract, ALU.mult)
                last.then_inc(v_xh3, 1)
                dve.wait_ge(v_xh3, g.n + 1)
                vv.scalar_tensor_tensor(HN[:], XH3[:], 0.0, per_graph(DN[:, g.slot, 8:12]), ALU.max,
                                        ALU.mult).then_inc(v_hn, 1)

            def l3_in(g):
                dve.wait_ge(pe_hg, g.n + 1)
                vv.tensor_tensor(GP[:], bank(Q + 1), row("L3_gnn_b_t"),
                                 ALU.add).then_inc(v_gp, 1)
                dve.wait_ge(pe_fhom, g.n + 1)
                vv.tensor_tensor(FH[:], bank(Q + 2), per_graph(DN[:, g.slot, 8:12]), ALU.mult).then_inc(v_fh, 1)

            def l3_mix(g):
                dve.wait_ge(v_fh, g.n + 1)
                dve.wait_ge(a_het, g.n + 1)
                vv.tensor_tensor(FH[:], FH[:], HET[:], ALU.subtract).then_inc(v_dd, 1)
                dve.wait_ge(v_dd, g.n + 1)
                dve.wait_ge(a_gate, g.n + 1)
                vv.scalar_tensor_tensor(FH[:], GP[:], 1.0, FH[:], ALU.add, ALU.mult).then_inc(v_e2, 1)
                dve.wait_ge(v_e2, g.n + 1)
                vv.scalar_tensor_tensor(FH[:], FH[:], 0.5, HET[:], ALU.mult, ALU.add).then_inc(v_v1, 1)
                dve.wait_ge(v_v1, g.n + 1)
                vv.tensor_scalar(MN[:], FH[:], 0.0, None, ALU.min).then_inc(v_mn, 1)

            def l3_out(g):
                dve.wait_ge(a_ex, g.n + 1)
                vv.scalar_tensor_tensor(MN[:], FH[:], 0.0, MN[:], ALU.max, ALU.add).then_inc(v_el, 1)
                dve.wait_ge(v_el, g.n + 1)
                if not (isinstance(g.n, int) and g.n < 2):
                    dve.wait_ge(out_stored[(g.slot + 2) % 4], (g.turn + (1 if g.slot >= 2 else 0)) * 16)
                vv.scalar_tensor_tensor(OUT[:, g.slot % 2], MN[:], -1.0, X3[:, g.slot % 2], ALU.add,
                                        ALU.add).then_inc(v_out, 1)

            def one_step(turn, step):
                a, b, c, d = (group(turn, step, lag) for lag in range(4))
                if c:
                    x_conv(c)
                if d:
                    context(d)
                if c:
                    x_conv_low(c)
                if b:
                    message(b)
                    c1_low(b)
                if a:
                    degree(a)
                    bn0(a)
                if c:
                    new_gate(c)
                if a:
                    h0(a)
                if d:
                    x3(d)
                if c:
                    blend(c)
                if d:
                    h3(d)
                if a:
                    x1(a)
                if c:
                    x2(c)
                if d:
                    l3_in(d)
                    l3_mix(d)
                if b:
                    nmp_low(b)
                if d:
                    l3_out(d)
                if a:
                    h1_low(a)
                if c:
                    delta(c)
                    values(c)
                    diagonal(c)

            schedule(dve, one_step)

        @block.tensor
        def _(pe):
            mm = nc.tensor.matmul

            def mm3(o, weight, hi, lo, start, stop):
                wh, wl = weight
                mm(o, wh, hi, start=start, stop=False)
                mm(o, wh, lo, start=False, stop=False)
                return mm(o, wl, hi, start=False, stop=stop)

            def transposes(b, src):
                for j in range(G):
                    last = nc.tensor.transpose(bank(b)[:, j], src[:, j], ident)
                return last

            def h1_products(g):
                pe.wait_ge(a_h1H, g.n + 1)
                pe.wait_ge(v_h1L, g.n + 1)
                mm3(PS[:, S1, :], w("conv1", 0), flat(H1H[:, g.slot]), flat(H1L[:, g.slot]), True,
                    True).then_inc(pe_conv1, 1)
                pe.wait_ge(a_h1T, g.n + 1)
                if not (isinstance(g.n, int) and g.n < 2):
                    if g.has(2):
                        pe.wait_ge(v_den0, g.n - 1)
                    if g.has(2):
                        pe.wait_ge(v_cc, g.n - 1)
                wide = pair_wide(T6, D + 3)
                for j in range(G):
                    last = mm(wide[:, j], H1T[:, g.slot, j], WMSG[:], start=True, stop=True)
                last.then_inc(pe_msg, 1)

            def gru(g):
                s, p = g.slot, g.slot % 2
                if g.has(1):
                    pe.wait_ge(v_hlsr, g.n)
                h = (flat(H1H[:, s]), flat(H1L[:, s]))
                nm = (flat(NMH[:, p]), flat(NML[:, p]))
                xc = (flat(XCH[:]), flat(XCL[:]))
                mm3(PS[:, Q + 2, :], w("whh", 2), *h, True, True).then_inc(pe_hn, 1)
                mm3(PS[:, Q, :], w("whh", 0), *h, True, False)
                mm3(PS[:, Q + 1, :], w("whh", 1), *h, True, False)
                pe.wait_ge(a_nmH, g.n + 1)
                pe.wait_ge(v_nmL, g.n + 1)
                mm3(PS[:, Q, :], w("wih", 3), *nm, False, False)
                mm3(PS[:, Q + 1, :], w("wih", 4), *nm, False, False)
                mm3(PS[:, Q + 3, :], w("wih", 5), *nm, True, False)
                pe.wait_ge(a_xcH, g.n + 1)
                pe.wait_ge(v_xcL, g.n + 1)
                mm3(PS[:, Q, :], w("wih", 0), *xc, False, True).then_inc(pe_r, 1)
                mm3(PS[:, Q + 3, :], w("wih", 2), *xc, False, True).then_inc(pe_in, 1)
                mm3(PS[:, Q + 1, :], w("wih", 1), *xc, False, True).then_inc(pe_z, 1)

            def adj_t(g, b):
                pe.wait_ge(adj_in[g.slot], (g.turn + 1) * 16)
                if b:
                    pe.wait_ge(a_c1, b.n + 1)
                transposes(S1, ADJ[:, g.slot % 2]).then_inc(pe_adjT, 1)

            def agg0(g):
                pe.wait_ge(v_hp, g.n + 1)
                pe.wait_ge(p_adji, g.n + 1)
                for j in range(G):
                    last = mm(bank(S1)[:, j], HP[:, j], ADJI[:, j], start=True, stop=True)
                last.then_inc(pe_u0, 1)

            def y0(g):
                pe.wait_ge(a_u0, g.n + 1)
                for j in range(G):
                    last = mm(bank(S1)[:, j], UT[:, j], W0[:], start=True, stop=True)
                last.then_inc(pe_y0, 1)

            def h1_t(g):
                pe.wait_ge(a_xh1, g.n + 1)
                pe.wait_ge(v_t1, g.n + 1)
                transposes(S1, XH1).then_inc(pe_h1T, 1)

            def s_t(g):
                pe.wait_ge(v_slr, g.n + 1)
                pe.wait_ge(v_msgp, g.n + 1)
                for side, b in ((0, T6), (1, T7)):
                    for j in range(G):
                        last = nc.tensor.transpose(PS[0:5, b, j * N:(j + 1) * N], SLR[:, j, side, 0:5], ident)
                last.then_inc(pe_sT, 1)

            def distance(g):
                pe.wait_ge(a_sT, g.n + 1)
                for j in range(G):
                    last = mm(bank(T6)[:, j], LRT[0:5, 0, j], LRT[0:5, 1, j], start=True, stop=True)
                last.then_inc(pe_dist, 1)

            def nmp(g):
                pe.wait_ge(a_msg, g.n + 1)
                pe.wait_ge(p_at, g.n + 1)
                for j in range(G):
                    last = mm(bank(T6)[:, j], MSG[:, j], AT[:, j], start=True, stop=True)
                last.then_inc(pe_nmp, 1)

            centre_first = [PAD] + [k for k in range(TAPS) if k != PAD]

            def conv2(g, first, last_):
                if first == 0:
                    pe.wait_ge(a_c1H, g.n + 1)
                    pe.wait_ge(v_c1L, g.n + 1)
                    if g.has(1):
                        pe.wait_ge(v_xcp, g.n)
                o = bank(CONV)
                for i in range(first, last_):
                    k = centre_first[i]
                    off = k - PAD
                    skip = abs(off) // 2 * 2
                    n = N - skip
                    a = skip if off < 0 else 0
                    hi = C1H[:, :, a + off + PAD:a + off + PAD + n]
                    lo = C1L[:, :, a + off + PAD:a + off + PAD + n]
                    last = mm3(o[:, :, a:a + n], w("conv2", k), hi, lo, i == 0, i == TAPS - 1)
                if last_ == TAPS:
                    last.then_inc(pe_conv2, 1)

            def gru_t(g, b):
                pe.wait_ge(v_gt, g.n + 1)
                if b:
                    pe.wait_ge(a_sT, b.n + 1)
                transposes(T7, DH).then_inc(pe_gruT, 1)

            def h2_t(g):
                pe.wait_ge(a_xh2, g.n + 1)
                transposes(T7, XH2).then_inc(pe_h2T, 1)

            def similarity(g):
                pe.wait_ge(a_h2T, g.n + 1)
                pe.wait_ge(a_h2H, g.n + 1)
                for j in range(G):
                    last = mm(bank(T7)[:, j], H2T[:, j], H2T[:, j], start=True, stop=True)
                last.then_inc(pe_sim, 1)

            def values(g, d):
                pe.wait_ge(p_h2L, g.n + 1)
                if d:
                    pe.wait_ge(a_het, d.n + 1)
                    pe.wait_ge(v_gp, d.n + 1)
                    pe.wait_ge(v_fh, d.n + 1)
                wh, wl = w("wlsr", 0, 3)
                for j in range(G):
                    o = PS[:, Q + j, 0:3 * D]
                    mm(o, H2H[:, j], wh, start=True, stop=False)
                    mm(o, H2H[:, j], wl, start=False, stop=False)
                    last = mm(o, H2L[:, j], wh, start=False, stop=True)
                last.then_inc(pe_hlsr, 1)

            def context(g, b):
                pe.wait_ge(p_dl, g.n + 1)
                pe.wait_ge(v_hlsr, g.n + 1)
                pe.wait_ge(a_sim, g.n + 1)
                if b:
                    pe.wait_ge(v_nmL, b.n + 1)
                wide = pair_wide(T6, D + 1)
                for j in range(G):
                    mm(wide[:, j], DL[:, j], HLR[:, j, 0, 0:D + 1], start=True, stop=False)
                    last = mm(wide[:, j], DR[:, j], HLR[:, j, 2, 0:D + 1], start=False, stop=True)
                last.then_inc(pe_ctx, 1)

            def h3_products(g, c):
                pe.wait_ge(v_xh3, g.n + 1)
                if c:
                    pe.wait_ge(a_r, c.n + 1)
                    pe.wait_ge(a_z, c.n + 1)
                transposes(Q, XH3).then_inc(pe_h3T, 1)
                pe.wait_ge(v_hn, g.n + 1)
                for j in range(G):
                    last = mm(bank(Q + 1)[:, j], HN[:, j], ADJT[:, g.slot, j], start=True, stop=True)
                last.then_inc(pe_g3, 1)

            def l3(g, c):
                pe.wait_ge(a_g3, g.n + 1)
                if c:
                    pe.wait_ge(a_q2, c.n + 1)
                for j in range(G):
                    last = mm(bank(Q + 2)[:, j], G3T[:, j], THETA[:], start=True, stop=True)
                last.then_inc(pe_fhom, 1)
                pe.wait_ge(a_h3T, g.n + 1)
                for j in range(G):
                    mm(bank(Q)[:, j], H3T[:, j], WHET[:, 0:D], start=True, stop=True)
                    last = mm(bank(Q + 1)[:, j], H3T[:, j], WHET[:, D:2 * D], start=True, stop=True)
                last.then_inc(pe_hg, 1)

            pe.wait_ge(consts_in, 48)
            pe.wait_ge(weights_in, 64)
            pe.wait_ge(piece_lo, len(cuts))

            def one_step(turn, step):
                a, b, c, d = (group(turn, step, lag) for lag in range(4))
                if b:
                    h1_products(b)
                if c:
                    gru(c)
                if a:
                    adj_t(a, b)
                if b:
                    conv2(b, 0, 4)
                    s_t(b)
                if a:
                    agg0(a)
                if d:
                    h3_products(d, c)
                if b:
                    distance(b)
                if a:
                    y0(a)
                if c:
                    gru_t(c, b)
                if d:
                    l3(d, c)
                if b:
                    conv2(b, 4, 8)
                    nmp(b)
                if c:
                    h2_t(c)
                if b:
                    conv2(b, 8, 11)
                if a:
                    h1_t(a)
                if c:
                    similarity(c)
                    values(c, d)
                if b:
                    conv2(b, 11, TAPS)
                if c:
                    context(c, b)

            schedule(pe, one_step)


def kernel(**inputs):
    import concourse.bacc as bacc
    from concourse.bass_utils import run_bass_kernel_spmd

    def arr(name):
        return np.asarray(inputs[name])

    m, n = np.arange(N)[:, None], np.arange(N)[None, :]
    eye = np.ascontiguousarray(np.stack([m == n, m > n, m < n], axis=1).astype(np.float32))
    bih, bhh = arr("L1_gnn_b_ih").reshape(3, D), arr("L1_gnn_b_hh").reshape(3, D)
    arrays = {
        "x": arr("x"),
        "adj": arr("adj"),
        "eye": eye,
        "rows": np.concatenate([arr(r) for r in ROWS]),
        "cols": np.ascontiguousarray(np.stack(
            [arr("L1_gnn_" + c) for c in COLS[:8]] + [bih[0], bih[1], bih[2], bhh[0], bhh[1], bhh[2]], axis=1)),
        "w0": arr("L0_gnn_W"),
        "conv1T": np.ascontiguousarray(arr("L1_gnn_conv1_w")[:, :, 0].T),
        "conv2T": np.ascontiguousarray(arr("L1_gnn_conv2_w").transpose(1, 2, 0).reshape(D, TAPS * D)),
        "wmsgT": np.ascontiguousarray(np.concatenate([arr("L1_gnn_w_msg"), arr("L1_gnn_w_se")]).T),
        "wihT": np.ascontiguousarray(arr("L1_gnn_w_ih").T.reshape(2, D, 3 * D).transpose(1, 0, 2).reshape(D, 6 * D)),
        "whhT": np.ascontiguousarray(arr("L1_gnn_w_hh").T),
        "wlsrT": np.ascontiguousarray(np.concatenate([arr("L2_gnn_Wl"), arr("L2_gnn_Ws"), arr("L2_gnn_Wr")]).T),
        "whet": np.ascontiguousarray(np.concatenate([arr("L3_gnn_W_h"), arr("L3_gnn_W_t")], axis=1)),
        "theta": arr("L3_gnn_theta"),
    }
    nc = bacc.Bacc("TRN2", target_bir_lowering=False, num_devices=1)
    args, feeds = [], {}
    for name, a in arrays.items():
        feeds[f"in_{name}"] = a
        args.append(nc.dram_tensor(f"in_{name}", a.shape, F32, kind="ExternalInput").ap())
    args.append(nc.dram_tensor("out_0", (B, N, D), F32, kind="ExternalOutput").ap())
    build(nc, *args)
    r = run_bass_kernel_spmd(nc, [feeds], core_ids=[0])
    return r.results[0]["out_0"]
```

```python
from collections import namedtuple
from contextlib import ExitStack

import numpy as np

import concourse.bass as bass
from concourse import mybir

F32 = mybir.dt.float32
F32R = mybir.dt.float32r
ALU = mybir.AluOpType
ACT = mybir.ActivationFunctionType
AX_X = mybir.AxisListType.X

B, N, D = 128, 128, 128
G = 4
GROUPS = B // G
LAGS = 4
ROUND = 4
TAPS = 17
SHARE = 3
PAD = TAPS // 2
LN_EPS = 1e-5
L2_LN_EPS = 1e-12
L2_RENORM_EPS = 1e-10
L3_DEG_EPS = 1e-6
BN_EPS = 1e-5

ROWS = ("L0_gnn_b", "L1_gnn_b_msg", "L1_gnn_b_se", "L2_gnn_bl", "L2_gnn_bs", "L2_gnn_br",
        "L2_gnn_ln_w", "L2_gnn_ln_b", "L3_gnn_b_t")
ROW_SIZE = {"L1_gnn_b_se": 3}
ROW_AT = {}
_at = 0
for _name in ROWS:
    ROW_AT[_name] = _at
    _at += ROW_SIZE.get(_name, D)
ROW_TOTAL = _at
COLS = ("bn1_g", "bn1_b", "bn1_m", "bn1_v", "bn2_g", "bn2_b", "bn2_m", "bn2_v",
        "bih_r", "bih_z", "bih_n", "bhh_r", "bhh_z", "bhh_n")
COL_AT = {n: i for i, n in enumerate(COLS)}

class Group(namedtuple("Group", "n slot turn")):
    def has(self, back):
        return not isinstance(self.n, int) or 0 <= self.n - back < GROUPS


def group(turn, step, lag):
    s = step - lag
    if isinstance(turn, int) and not 0 <= turn * ROUND + s < GROUPS:
        return None
    return Group(turn * ROUND + s, s % ROUND, turn + s // ROUND)


def build(nc, x, adj, eye, rows, cols, w0, conv1T, conv2T, wmsgT, wihT, whhT, wlsrT, whet, theta, out):
    ctx = ExitStack()

    def sb(name, shape, dt=F32):
        return ctx.enter_context(nc.sbuf_tensor(name, [128, *shape], dt))

    def sem(name):
        return ctx.enter_context(nc.semaphore(name))

    with ctx:
        PS = ctx.enter_context(nc.psum_tensor("banks", [128, 8, 512], F32))

        def bank(b, n=1):
            return PS[:, b:b + n, :].rearrange("p b (g n) -> p (b g) n", n=N)

        def pair_wide(b, w):
            return PS[:, b:b + 2, :].rearrange("p b (g n) -> p (b g) n", n=256)[:, :, 0:w]

        B0, B1, B2, B3, B4, B5, B6, B7 = range(8)

        EYE = sb("EYE", [3, N])
        ROWV = sb("ROWV", [ROW_TOTAL])
        COLV = sb("COLV", [len(COLS)])
        CW = sb("CW", [8])
        CG = sb("CG", [4])
        CT = sb("CT", [8])
        W0 = sb("W0", [D])
        WMSG = sb("WMSG", [D + 3])
        WHET = sb("WHET", [2 * D])
        THETA = sb("THETA", [D])
        NSPLIT = TAPS * D + D + 2 * 3 * D + 3 * D + 3 * D
        WF = sb("WF", [3 * D])
        WHI = sb("WHI", [NSPLIT], F32R)
        WLO = sb("WLO", [NSPLIT], F32R)
        MHALF = sb("MHALF", [12])
        EPS = sb("EPS", [8])
        at = 0
        where = {}
        for name, size in (("conv2", TAPS * D), ("conv1", D), ("wih", 6 * D), ("whh", 3 * D), ("wlsr", 3 * D)):
            where[name] = at
            at += size

        def w(name, c, n=1):
            a = where[name] + c * D
            return WHI[:, a:a + n * D], WLO[:, a:a + n * D]

        X = sb("X", [2, G, D])
        ADJ = sb("ADJ", [2, G, N])
        ADJT = sb("ADJT", [4, G, N])
        ADJI = sb("ADJI", [G, N])
        XB = sb("XB", [G, D])
        DEG = sb("DEG", [4, G])
        ST = [sb(f"ST{k}", [G, 6]) for k in range(5)]
        MV = [sb(f"MV{k}", [2, G, 2]) for k in range(5)]
        NM = [sb(f"NM{k}", [2, G]) for k in range(5)]
        VE = [sb(f"VE{k}", [2, G]) for k in range(5)]
        RS = [sb(f"RS{k}", [2, G]) for k in range(5)]
        NR = [sb(f"NR{k}", [2, G]) for k in range(5)]
        PW = sb("PW", [2, 12])
        ZD = sb("ZD", [G])
        KEEP = sb("KEEP", [2, G])
        SC0, BI0, SC3, BI3 = [sb(n, [2, G]) for n in ("SC0", "BI0", "SC3", "BI3")]
        ONE = sb("ONE", [1])
        DN = sb("DN", [4, 12])
        HP = sb("HP", [G, D])
        UT = sb("UT", [G, N])
        X1 = sb("X1", [4, G, D])
        XH1 = sb("XH1", [G, D])
        H1T = sb("H1T", [4, G, N])
        H1H = sb("H1H", [4, G, N], F32R)
        H1L = sb("H1L", [4, G, N], F32R)
        C1 = sb("C1", [G, N])
        C1H = sb("C1H", [G, N + 2 * PAD], F32R)
        C1L = sb("C1L", [G, N + 2 * PAD], F32R)
        MSG = sb("MSG", [G, D])
        SS = sb("SS", [G, 3])
        SLR = sb("SLR", [G, 2, 8])
        LRT = ctx.enter_context(nc.sbuf_tensor("LRT", [8, 2, G, N], F32))
        EA = sb("EA", [G, N])
        AT = sb("AT", [G, N])
        NMH = sb("NMH", [2, G, N], F32R)
        NML = sb("NML", [2, G, N], F32R)
        XCP = sb("XCP", [G, N])
        XCH = sb("XCH", [G, N], F32R)
        XCL = sb("XCL", [G, N], F32R)
        TR = sb("TR", [G, N])
        TZ = sb("TZ", [G, N])
        Q2 = sb("Q2", [G, N])
        DH = sb("DH", [G, N])
        X2 = sb("X2", [2, G, D])
        XH2 = sb("XH2", [G, D])
        H2T = sb("H2T", [G, N])
        H2H = sb("H2H", [G, N], F32R)
        H2L = sb("H2L", [G, N], F32R)
        EE = sb("EE", [G, N])
        DE = sb("DE", [G, N])
        DL = sb("DL", [G, N])
        DR = sb("DR", [G, N])
        DI = sb("DI", [G, N])
        ZS = sb("ZS", [2, G])
        DG = sb("DG", [2, G])
        HLR = sb("HLR", [G, 3, D + 4])
        HSD = sb("HSD", [G, D])
        CC = sb("CC", [G, D])
        DEN = sb("DEN", [2, 2, G])
        CH = sb("CH", [G, D])
        X3 = sb("X3", [2, G, D])
        XH3 = sb("XH3", [G, D])
        HN = sb("HN", [G, D])
        H3T = sb("H3T", [G, N])
        G3T = sb("G3T", [G, N])
        X3M = sb("X3M", [2, G, D])
        HET = sb("HET", [G, D])
        FH = sb("FH", [G, D])
        GP = sb("GP", [G, D])
        EX = sb("EX", [G, D])
        OUT = sb("OUT", [2, G, D])

        x_in = [sem(f"x_in{s}") for s in range(4)]
        adj_in = [sem(f"adj_in{s}") for s in range(4)]
        out_stored = [sem(f"out_stored{s}") for s in range(4)]
        consts_in = sem("consts_in")
        weights_in = sem("weights_in")
        pieces_in = [sem(f"piece_in{k}") for k in range(5)]
        piece_hi = sem("piece_hi")
        piece_lo = sem("piece_lo")
        consts_pool = sem("consts_pool")
        consts_ready = sem("consts_ready")
        (pe_conv1, pe_msg, pe_gruH, pe_gruN, pe_gruX, pe_adjT, pe_h3T, pe_g3, pe_sT, pe_u0, pe_hg, pe_fhom,
         pe_dist, pe_y0, pe_gruT, pe_nmp, pe_h2T, pe_h1T, pe_sim, pe_hl, pe_conv2, pe_ctx) = [
            sem("pe_" + s) for s in
            "conv1 msg gruH gruN gruX adjT h3T g3 sT u0 hg fhom dist y0 gruT nmp h2T h1T sim hl conv2 ctx".split()]
        (a_adjT, a_hp, a_u0, a_yd, a_xh1, a_h1T, a_h1H, a_c1, a_c1H, a_msg, a_sT, a_exp, a_nmH, a_xcH, a_r,
         a_q2, a_z, a_nn, a_xh2, a_h2T, a_h2H, a_sim, a_ch, a_xh3, a_hn3, a_h3T, a_g3, a_fh, a_het, a_gate,
         a_ex) = [sem("a_" + s) for s in
                  ("adjT hp u0 yd xh1 h1T h1H c1 c1H msg sT exp nmH xcH r q2 z nn xh2 h2T h2H sim ch xh3 hn3 "
                   "h3T g3 fh het gate ex").split()]
        (v_sum, v_zd, v_deg, v_x1, v_c1L, v_msgp, v_s, v_s2, v_slr, v_nmL, v_xcp, v_xc, v_xcL, v_rq, v_ni,
         v_dh0, v_dh1, v_dh, v_x2, v_hl, v_de, v_zs, v_diag, v_cc, v_den0, v_den, v_x3, v_gp, v_mix0, v_mix1,
         v_mix, v_out0, v_out) = [sem("v_" + s) for s in
                                  ("sum zd deg x1 c1L msgp s s2 slr nmL xcp xc xcL rq ni dh0 dh1 dh x2 hl de zs "
                                   "diag cc den0 den x3 gp mix0 mix1 mix out0 out").split()]
        v_st, v_nm, v_bn = [[sem(f"v_{s}{k}") for k in range(5)] for s in ("st", "nm", "bn")]
        p_ve, p_pw, p_rs = [[sem(f"p_{s}{k}") for k in range(5)] for s in ("ve", "pw", "rs")]
        (p_keep, p_sc0, p_sc3, p_adji, p_xb, p_h1L, p_at, p_h2L, p_dl, p_di, p_hsd, p_d2, p_d3, p_lnw, p_lnb,
         p_x3m) = [sem("p_" + s) for s in
                   "keep sc0 sc3 adji xb h1L at h2L dl di hsd d2 d3 lnw lnb x3m".split()]

        def row(name):
            n = ROW_SIZE.get(name, D)
            return ROWV[:, ROW_AT[name]:ROW_AT[name] + n].unsqueeze(1).to_broadcast([128, G, n])

        def per_graph(v):
            return v.unsqueeze(2).to_broadcast([128, G, D])

        def mask(k):
            return EYE[:, k, :].unsqueeze(1).to_broadcast([128, G, N])

        def flat(t):
            return t.rearrange("p g n -> p (g n)")

        ident = EYE[:, 0, :]
        x_d = x.rearrange("(s g) n d -> s n g d", g=G)
        adj_d = adj.rearrange("(s g) n m -> s n g m", g=G)
        out_d = out.rearrange("(s g) n d -> s n g d", g=G)

        def schedule(engine, one_step):
            for step in range(ROUND):
                one_step(0, step)
            with engine.Fori(1, GROUPS // ROUND) as turn:
                for step in range(ROUND):
                    one_step(turn, step)
            for step in range(LAGS - 1):
                one_step(GROUPS // ROUND, step)

        pieces = (("conv1", conv1T, 1), ("wih", wihT, 6), ("whh", whhT, 3), ("wlsr", wlsrT, 3),
                  ("conv2", conv2T, TAPS))
        PIECE = 3
        cuts = [(name, src, c, min(PIECE, n - c)) for name, src, n in pieces for c in range(0, n, PIECE)]
        block = ctx.enter_context(nc.Block())

        @block.sync
        def _(sp):
            sp.dma_start(EYE[:], eye).then_inc(consts_in, 16)
            sp.dma_start(COLV[:], cols).then_inc(consts_in, 16)
            sp.dma_start(ROWV[:], rows.partition_broadcast(128)).then_inc(consts_in, 16)

            def load(g):
                if g.has(2):
                    sp.wait_ge(p_xb, g.n - 1)
                    sp.wait_ge(a_hp, g.n - 1)
                sp.dma_start(X[:, g.slot % 2], x_d[g.n]).then_inc(x_in[g.slot], 16)
                if g.has(2):
                    sp.wait_ge(pe_adjT, g.n - 1)
                    sp.wait_ge(v_sum, g.n - 1)
                sp.dma_start(ADJ[:, g.slot % 2], adj_d[g.n]).then_inc(adj_in[g.slot], 16)

            def store(g):
                sp.wait_ge(v_out, g.n + 1)
                sp.dma_start(out_d[g.n], OUT[:, g.slot % 2]).then_inc(out_stored[g.slot], 16)

            def weights():
                sp.dma_start(W0[:], w0).then_inc(weights_in, 16)
                sp.dma_start(WMSG[:], wmsgT).then_inc(weights_in, 16)
                sp.dma_start(WHET[:], whet).then_inc(weights_in, 16)
                sp.dma_start(THETA[:], theta).then_inc(weights_in, 16)
                for k, (name, src, c, n) in enumerate(cuts):
                    if k:
                        sp.wait_ge(piece_lo, k)
                    sp.dma_start(WF[:, 0:n * D], src[:, c * D:(c + n) * D]).then_inc(pieces_in[0], 16)

            def one_step(turn, step):
                g, d = group(turn, step, -1), group(turn, step, LAGS - 1)
                if isinstance(turn, int) and turn == 0 and step == 0:
                    load(group(0, 0, 0))
                    load(group(0, 1, 0))
                    weights()
                elif g is not None and (not isinstance(turn, int) or turn * ROUND + step + 1 < GROUPS):
                    load(g)
                if d is not None:
                    store(d)

            for step in range(ROUND):
                one_step(0, step)
            with sp.Fori(1, GROUPS // ROUND - 1) as turn:
                for step in range(ROUND):
                    one_step(turn, step)
            for step in range(ROUND):
                one_step(GROUPS // ROUND - 1, step)
            for step in range(LAGS - 1):
                one_step(GROUPS // ROUND, step)
            for s in range(4):
                sp.wait_ge(out_stored[s], 16 * (GROUPS // 4))

        @block.gpsimd
        def _(pool):
            pp = nc.gpsimd
            links = [0]

            def small(ins):
                links[0] += 1
                ins.then_inc(consts_pool, 1)
                pool.wait_ge(consts_pool, links[0])

            def col(n):
                return COLV[:, COL_AT[n]:COL_AT[n] + 1]

            small(pp.memset(MHALF[:], -0.5))
            small(pp.memset(ONE[:], 1.0))
            small(pp.memset(EPS[:, 0:4], LN_EPS))
            small(pp.memset(EPS[:, 4:8], L2_LN_EPS))
            small(pp.memset(HLR[:], 1.0))
            small(pp.memset(SLR[:], 1.0))
            small(pp.memset(C1H[:].bitcast(F32), 0.0))
            small(pp.memset(C1L[:].bitcast(F32), 0.0))
            pool.wait_ge(consts_in, 48)
            for k in (0, 1):
                bn = f"bn{k + 1}_"
                small(pp.tensor_scalar(CT[:, 0:1], col(bn + "v"), BN_EPS, None, ALU.add))
                small(pp.tensor_tensor(CT[:, 1:2], CT[:, 0:1], MHALF[:, 0:1], ALU.pow))
                small(pp.tensor_tensor(CW[:, 2 * k:2 * k + 1], CT[:, 1:2], col(bn + "g"), ALU.mult))
                small(pp.tensor_tensor(CT[:, 2:3], CW[:, 2 * k:2 * k + 1], col(bn + "m"), ALU.mult))
                small(pp.tensor_tensor(CW[:, 2 * k + 1:2 * k + 2], col(bn + "b"), CT[:, 2:3], ALU.subtract))
            for k, gate in enumerate("rz"):
                small(pp.tensor_tensor(CT[:, 3:4], col("bih_" + gate), col("bhh_" + gate), ALU.add))
                small(pp.tensor_scalar(CG[:, k:k + 1], CT[:, 3:4], 0.5, None, ALU.mult))
            small(pp.tensor_scalar(CG[:, 2:3], col("bhh_n"), 0.5, None, ALU.mult))
            pp.tensor_copy(CG[:, 3:4], col("bih_n")).then_inc(consts_ready, 1)

            def pw0(g):
                s, p = g.slot, g.slot % 2
                pool.wait_ge(v_bn[0], g.n + 1)
                pp.tensor_tensor(PW[:, p, 0:4], MV[0][:, p, :, 1], EPS[:, 0:4], ALU.add).then_inc(p_ve[0], 1)
                pool.wait_ge(v_deg, g.n + 1)
                pool.wait_ge(p_ve[0], g.n + 1)
                pp.tensor_tensor(DN[:, s], PW[:, p], MHALF[:], ALU.pow).then_inc(p_pw[0], 1)
                pool.wait_ge(p_pw[0], g.n + 1)
                pp.tensor_tensor(DN[:, s, 4:8], DN[:, s, 4:8], KEEP[:, p], ALU.mult).then_inc(p_keep, 1)
                pool.wait_ge(p_keep, g.n + 1)
                pp.tensor_tensor(SC0[:, p], DN[:, s, 0:4], DN[:, s, 4:8], ALU.mult).then_inc(p_sc0, 1)
                pool.wait_ge(p_sc0, g.n + 1)
                pp.tensor_tensor(BI0[:, p], NM[0][:, p], SC0[:, p], ALU.mult).then_inc(p_rs[0], 1)

            def rstd(k, g):
                p = g.slot % 2
                pool.wait_ge(v_bn[k], g.n + 1)
                pp.tensor_tensor(VE[k][:, p], MV[k][:, p, :, 1], EPS[:, 0:4], ALU.add).then_inc(p_ve[k], 1)
                pool.wait_ge(p_ve[k], g.n + 1)
                pp.tensor_tensor(RS[k][:, p], VE[k][:, p], MHALF[:, 0:4], ALU.pow).then_inc(p_pw[k], 1)
                pool.wait_ge(p_pw[k], g.n + 1)
                return pp.tensor_tensor(NR[k][:, p], NM[k][:, p], RS[k][:, p], ALU.mult)

            def rs1(g):
                rstd(1, g).then_inc(p_rs[1], 1)

            def rs2(g):
                rstd(2, g).then_inc(p_rs[2], 1)

            def rs3(g):
                p = g.slot % 2
                rstd(3, g)
                pp.tensor_tensor(SC3[:, p], RS[3][:, p], DN[:, g.slot, 8:12], ALU.mult).then_inc(p_sc3, 1)
                pool.wait_ge(p_sc3, g.n + 1)
                pp.tensor_tensor(BI3[:, p], NM[3][:, p], SC3[:, p], ALU.mult).then_inc(p_rs[3], 1)

            def rs4(g):
                p = g.slot % 2
                pool.wait_ge(v_den, g.n + 1)
                pp.tensor_tensor(DEN[:, 0, p], DEN[:, 1, p], DEN[:, 1, p], ALU.mult).then_inc(p_d2, 1)
                pool.wait_ge(p_d2, g.n + 1)
                pp.tensor_tensor(VE[4][:, p], DEN[:, 0, p], EPS[:, 4:8], ALU.mult).then_inc(p_d3, 1)
                pool.wait_ge(p_d3, g.n + 1)
                pool.wait_ge(v_bn[4], g.n + 1)
                pp.tensor_tensor(DEN[:, 0, p], VE[4][:, p], MV[4][:, p, :, 1], ALU.add).then_inc(p_ve[4], 1)
                pool.wait_ge(p_ve[4], g.n + 1)
                pp.tensor_tensor(RS[4][:, p], DEN[:, 0, p], MHALF[:, 0:4], ALU.pow).then_inc(p_pw[4], 1)
                pool.wait_ge(p_pw[4], g.n + 1)
                pp.tensor_tensor(NR[4][:, p], NM[4][:, p], RS[4][:, p], ALU.mult).then_inc(p_rs[4], 1)

            def adji(g):
                pool.wait_ge(a_adjT, g.n + 1)
                pp.tensor_tensor(ADJI[:], ADJT[:, g.slot], mask(0), ALU.add).then_inc(p_adji, 1)

            def xb(g):
                pool.wait_ge(x_in[g.slot], (g.turn + 1) * 16)
                pp.tensor_tensor(XB[:], X[:, g.slot % 2], row("L0_gnn_b"), ALU.add).then_inc(p_xb, 1)

            def h1L(g):
                pool.wait_ge(a_h1T, g.n + 1)
                pool.wait_ge(a_h1H, g.n + 1)
                pp.tensor_tensor(H1L[:, g.slot], H1T[:, g.slot], H1H[:, g.slot].bitcast(F32),
                                 ALU.subtract).then_inc(p_h1L, 1)

            def at(g):
                pool.wait_ge(a_exp, g.n + 1)
                pp.tensor_tensor(AT[:], EA[:], ADJT[:, g.slot], ALU.mult).then_inc(p_at, 1)

            def h2L(g):
                pool.wait_ge(a_h2T, g.n + 1)
                pool.wait_ge(a_h2H, g.n + 1)
                pp.tensor_tensor(H2L[:], H2T[:], H2H[:].bitcast(F32), ALU.subtract).then_inc(p_h2L, 1)

            def dl(g):
                pool.wait_ge(v_de, g.n + 1)
                pp.tensor_tensor(DL[:], DE[:], mask(1), ALU.mult)
                pp.tensor_tensor(DR[:], DE[:], mask(2), ALU.mult).then_inc(p_dl, 1)

            def di(g):
                pool.wait_ge(v_de, g.n + 1)
                pp.tensor_tensor(DI[:], DE[:], mask(0), ALU.mult).then_inc(p_di, 1)

            def hsd(g):
                pool.wait_ge(v_diag, g.n + 1)
                pool.wait_ge(v_hl, g.n + 1)
                pp.tensor_tensor(HSD[:], HLR[:, :, 1, 0:D], per_graph(DG[:, g.slot % 2]),
                                 ALU.mult).then_inc(p_hsd, 1)

            def lnw(g):
                pool.wait_ge(a_ch, g.n + 1)
                pp.tensor_tensor(CH[:], CH[:], row("L2_gnn_ln_w"), ALU.mult).then_inc(p_lnw, 1)

            def lnb(g):
                pool.wait_ge(p_lnw, g.n + 1)
                pp.tensor_tensor(CH[:], CH[:], row("L2_gnn_ln_b"), ALU.add).then_inc(p_lnb, 1)

            def x3m(g):
                pool.wait_ge(v_x3, g.n + 1)
                pp.tensor_tensor(X3M[:, g.slot % 2], X3[:, g.slot % 2],
                                 ONE[:].unsqueeze(2).to_broadcast([128, G, D]), ALU.subtract).then_inc(p_x3m, 1)

            def one_step(turn, step):
                a, b, c, d = (group(turn, step, lag) for lag in range(LAGS))
                if a:
                    pw0(a)
                if d:
                    rs3(d)
                if a:
                    adji(a)
                if c:
                    rs2(c)
                if b:
                    at(b)
                if a:
                    xb(a)
                if d:
                    x3m(d)
                if c:
                    h2L(c)
                if a:
                    rs1(a)
                if c:
                    di(c)
                    dl(c)
                    hsd(c)
                if a:
                    h1L(a)
                if c:
                    rs4(c)
                    lnw(c)
                    lnb(c)

            schedule(pool, one_step)

        @block.scalar
        def _(act):
            aa = nc.scalar.activation
            act.wait_ge(consts_ready, 1)

            def affine(dst, src, scale, bias, func):
                for j in range(G):
                    last = aa(dst[:, j], src[:, j], func, scale=scale[:, j:j + 1], bias=bias[:, j:j + 1])
                return last

            def scaled(dst, src, scale):
                for j in range(G):
                    last = aa(dst[:, j], src[:, j], ACT.Copy, scale=scale[:, j:j + 1])
                return last

            def hp(g):
                p = g.slot % 2
                act.wait_ge(p_rs[0], g.n + 1)
                affine(HP, X[:, p], SC0[:, p], BI0[:, p], ACT.Relu).then_inc(a_hp, 1)

            def adjTe(g):
                act.wait_ge(pe_adjT, g.n + 1)
                aa(ADJT[:, g.slot], bank(B5), ACT.Copy).then_inc(a_adjT, 1)

            def u0e(g):
                act.wait_ge(pe_u0, g.n + 1)
                aa(UT[:], bank(B5), ACT.Copy).then_inc(a_u0, 1)

            def yd(g):
                act.wait_ge(pe_y0, g.n + 1)
                act.wait_ge(p_rs[0], g.n + 1)
                scaled(X1[:, g.slot], bank(B5), DN[:, g.slot, 4:8]).then_inc(a_yd, 1)

            def xh1(g):
                p = g.slot % 2
                act.wait_ge(p_rs[1], g.n + 1)
                affine(XH1, X1[:, g.slot], RS[1][:, p], NR[1][:, p], ACT.Relu).then_inc(a_xh1, 1)

            def h1Te(g):
                act.wait_ge(pe_h1T, g.n + 1)
                aa(H1T[:, g.slot], bank(B5), ACT.Copy).then_inc(a_h1T, 1)

            def h1H(g):
                act.wait_ge(pe_h1T, g.n + 1)
                aa(H1H[:, g.slot], bank(B5), ACT.Copy).then_inc(a_h1H, 1)

            def c1(g):
                act.wait_ge(pe_conv1, g.n + 1)
                aa(C1[:], bank(B5), ACT.Relu, scale=CW[:, 0:1], bias=CW[:, 1:2]).then_inc(a_c1, 1)

            def c1H(g):
                act.wait_ge(a_c1, g.n + 1)
                aa(C1H[:, :, PAD:PAD + N], C1[:], ACT.Copy).then_inc(a_c1H, 1)

            def msgr(g):
                act.wait_ge(v_msgp, g.n + 1)
                aa(MSG[:], MSG[:], ACT.Relu).then_inc(a_msg, 1)

            def sTe(g):
                act.wait_ge(pe_sT, g.n + 1)
                aa(LRT[0:5].rearrange("p l g n -> p l (g n)"), PS[0:5, B6:B7 + 1, :], ACT.Copy).then_inc(a_sT, 1)

            def exp(g):
                act.wait_ge(pe_dist, g.n + 1)
                aa(EA[:], bank(B6), ACT.Exp).then_inc(a_exp, 1)

            def nmH(g):
                act.wait_ge(pe_nmp, g.n + 1)
                aa(NMH[:, g.slot % 2], bank(B6), ACT.Copy).then_inc(a_nmH, 1)

            def xcH(g):
                act.wait_ge(v_xc, g.n + 1)
                aa(XCH[:], XCP[:], ACT.Copy).then_inc(a_xcH, 1)

            def q2(g):
                act.wait_ge(pe_gruH, g.n + 1)
                aa(Q2[:], bank(B3), ACT.Identity, scale=0.5, bias=CG[:, 2:3]).then_inc(a_q2, 1)

            def r(g):
                act.wait_ge(pe_gruX, g.n + 1)
                aa(TR[:], bank(B1), ACT.Tanh, scale=0.5, bias=CG[:, 0:1]).then_inc(a_r, 1)

            def z(g):
                act.wait_ge(pe_gruX, g.n + 1)
                aa(TZ[:], bank(B2), ACT.Tanh, scale=0.5, bias=CG[:, 1:2]).then_inc(a_z, 1)

            def nn(g):
                act.wait_ge(v_ni, g.n + 1)
                aa(Q2[:], Q2[:], ACT.Tanh, bias=CG[:, 3:4]).then_inc(a_nn, 1)

            def xh2(g):
                p = g.slot % 2
                act.wait_ge(p_rs[2], g.n + 1)
                affine(XH2, X2[:, p], RS[2][:, p], NR[2][:, p], ACT.Relu).then_inc(a_xh2, 1)

            def h2Te(g):
                act.wait_ge(pe_h2T, g.n + 1)
                aa(H2T[:], bank(B7), ACT.Copy).then_inc(a_h2T, 1)

            def h2H(g):
                act.wait_ge(pe_h2T, g.n + 1)
                aa(H2H[:], bank(B7), ACT.Copy).then_inc(a_h2H, 1)

            def simE(g):
                act.wait_ge(pe_sim, g.n + 1)
                aa(EE[:], bank(B7), ACT.Exp, scale=float(D) ** -0.5).then_inc(a_sim, 1)

            def ch(g):
                p = g.slot % 2
                act.wait_ge(p_rs[4], g.n + 1)
                affine(CH, CC, RS[4][:, p], NR[4][:, p], ACT.Identity).then_inc(a_ch, 1)

            def xh3(g):
                p = g.slot % 2
                act.wait_ge(p_rs[3], g.n + 1)
                affine(XH3, X3[:, p], RS[3][:, p], NR[3][:, p], ACT.Relu).then_inc(a_xh3, 1)

            def hn3(g):
                p = g.slot % 2
                act.wait_ge(p_rs[3], g.n + 1)
                affine(HN, X3[:, p], SC3[:, p], BI3[:, p], ACT.Relu).then_inc(a_hn3, 1)

            def h3Te(g):
                act.wait_ge(pe_h3T, g.n + 1)
                aa(H3T[:], bank(B1), ACT.Copy).then_inc(a_h3T, 1)

            def g3e(g):
                act.wait_ge(pe_g3, g.n + 1)
                aa(G3T[:], bank(B2), ACT.Copy).then_inc(a_g3, 1)

            def fh(g):
                act.wait_ge(pe_fhom, g.n + 1)
                scaled(FH, bank(B3), DN[:, g.slot, 8:12]).then_inc(a_fh, 1)

            def hete(g):
                act.wait_ge(pe_hg, g.n + 1)
                aa(HET[:], bank(B1), ACT.Copy).then_inc(a_het, 1)

            def gate(g):
                act.wait_ge(v_gp, g.n + 1)
                aa(GP[:], GP[:], ACT.Tanh, scale=0.5).then_inc(a_gate, 1)

            def ex(g):
                act.wait_ge(v_mix, g.n + 1)
                aa(EX[:], FH[:], ACT.Exp).then_inc(a_ex, 1)

            def one_step(turn, step):
                a, b, c, d = (group(turn, step, lag) for lag in range(LAGS))
                if a:
                    adjTe(a)
                if c:
                    nn(c)
                    z(c)
                if b:
                    sTe(b)
                if a:
                    hp(a)
                if b:
                    msgr(b)
                if d:
                    hn3(d)
                    xh3(d)
                    g3e(d)
                if a:
                    u0e(a)
                if d:
                    h3Te(d)
                if b:
                    exp(b)
                if c:
                    xh2(c)
                if a:
                    yd(a)
                if c:
                    h2H(c)
                    h2Te(c)
                if b:
                    nmH(b)
                if d:
                    fh(d)
                    hete(d)
                if c:
                    simE(c)
                if d:
                    gate(d)
                if a:
                    xh1(a)
                    h1Te(a)
                if d:
                    ex(d)
                if a:
                    h1H(a)
                if b:
                    q2(b)
                if a:
                    c1(a)
                if b:
                    xcH(b)
                if a:
                    c1H(a)
                if c:
                    ch(c)
                if b:
                    r(b)

            schedule(act, one_step)

        @block.vector
        def _(dve):
            vv = nc.vector
            for k, (name, src, c, n) in enumerate(cuts):
                hi, lo = w(name, c, n)
                dve.wait_ge(pieces_in[0], 16 * (k + 1))
                vv.tensor_copy(hi, WF[:, 0:n * D]).then_inc(piece_hi, 1)
                dve.wait_ge(piece_hi, k + 1)
                vv.tensor_tensor(lo, WF[:, 0:n * D], hi.bitcast(F32), ALU.subtract).then_inc(piece_lo, 1)
            dve.wait_ge(consts_ready, 1)

            def stats(k, g, src):
                p = g.slot % 2
                for j in range(G):
                    last = vv.bn_stats(ST[k][:, j], src[:, j])
                last.then_inc(v_st[k], 1)
                dve.wait_ge(v_st[k], g.n + 1)
                vv.tensor_scalar(NM[k][:, p], ST[k][:, :, 1], -0.5, None, ALU.mult).then_inc(v_nm[k], 1)
                for j in range(G):
                    vv.bn_aggr(MV[k][:, p, j], ST[k][:, j])
                dve.wait_ge(v_nm[k], g.n + 1)
                return vv.scalar_tensor_tensor(NM[k][:, p], ST[k][:, :, 4], -0.5, NM[k][:, p], ALU.mult, ALU.add)

            def deg(g):
                p = g.slot % 2
                sums = DEG[:, g.slot]
                dve.wait_ge(adj_in[g.slot], (g.turn + 1) * 16)
                vv.tensor_reduce(sums, ADJ[:, p], AX_X, ALU.add).then_inc(v_sum, 1)
                dve.wait_ge(v_sum, g.n + 1)
                vv.tensor_scalar(ZD[:], sums, 1.0, 0.0, ALU.add, ALU.is_equal).then_inc(v_zd, 1)
                vv.tensor_scalar(KEEP[:, p], sums, 1.0, 0.0, ALU.add, ALU.not_equal)
                vv.tensor_scalar(PW[:, p, 8:12], sums, L3_DEG_EPS, None, ALU.add)
                dve.wait_ge(v_zd, g.n + 1)
                vv.scalar_tensor_tensor(PW[:, p, 4:8], sums, 1.0, ZD[:], ALU.add, ALU.add).then_inc(v_deg, 1)

            def bn0(g):
                dve.wait_ge(x_in[g.slot], (g.turn + 1) * 16)
                stats(0, g, X[:, g.slot % 2]).then_inc(v_bn[0], 1)

            def x1(g):
                s = g.slot
                dve.wait_ge(a_yd, g.n + 1)
                dve.wait_ge(p_xb, g.n + 1)
                vv.tensor_tensor(X1[:, s], X1[:, s], XB[:], ALU.add).then_inc(v_x1, 1)

            def bn1(g):
                dve.wait_ge(v_x1, g.n + 1)
                stats(1, g, X1[:, g.slot]).then_inc(v_bn[1], 1)

            def c1L(g):
                dve.wait_ge(a_c1H, g.n + 1)
                vv.tensor_tensor(C1L[:, :, PAD:PAD + N], C1[:], C1H[:, :, PAD:PAD + N].bitcast(F32),
                                 ALU.subtract).then_inc(v_c1L, 1)

            def msgp(g):
                dve.wait_ge(pe_msg, g.n + 1)
                vv.tensor_tensor(MSG[:], pair_wide(B6, D + 3)[:, :, 0:D], row("L1_gnn_b_msg"),
                                 ALU.add).then_inc(v_msgp, 1)

            def s(g):
                left, right = SLR[:, :, 0], SLR[:, :, 1]
                dve.wait_ge(pe_msg, g.n + 1)
                vv.tensor_tensor(right[:, :, 0:3], pair_wide(B6, D + 3)[:, :, D:D + 3], row("L1_gnn_b_se"),
                                 ALU.add).then_inc(v_s, 1)
                dve.wait_ge(v_s, g.n + 1)
                vv.tensor_tensor(SS[:], right[:, :, 0:3], right[:, :, 0:3], ALU.mult).then_inc(v_s2, 1)
                vv.tensor_scalar(left[:, :, 0:3], right[:, :, 0:3], 2.0, None, ALU.mult)
                dve.wait_ge(v_s2, g.n + 1)
                vv.tensor_reduce(left[:, :, 3:4], SS[:], AX_X, ALU.add, negate=True)
                vv.tensor_reduce(right[:, :, 4:5], SS[:], AX_X, ALU.add, negate=True).then_inc(v_slr, 1)

            def nmL(g):
                dve.wait_ge(a_nmH, g.n + 1)
                vv.tensor_tensor(NML[:, g.slot % 2], bank(B6), NMH[:, g.slot % 2].bitcast(F32),
                                 ALU.subtract).then_inc(v_nmL, 1)

            def xc(g):
                dve.wait_ge(pe_conv2, g.n + 1)
                vv.scalar_tensor_tensor(flat(XCP[:]), flat(bank(B0)), CW[:, 2:3], flat(H1T[:, g.slot]),
                                        ALU.mult, ALU.add).then_inc(v_xcp, 1)
                dve.wait_ge(v_xcp, g.n + 1)
                vv.tensor_scalar(XCP[:], XCP[:], CW[:, 3:4], 0.0, ALU.add, ALU.max).then_inc(v_xc, 1)

            def xcL(g):
                dve.wait_ge(a_xcH, g.n + 1)
                vv.tensor_tensor(XCL[:], XCP[:], XCH[:].bitcast(F32), ALU.subtract).then_inc(v_xcL, 1)

            def ni(g):
                dve.wait_ge(a_q2, g.n + 1)
                dve.wait_ge(a_r, g.n + 1)
                vv.scalar_tensor_tensor(Q2[:], TR[:], 1.0, Q2[:], ALU.add, ALU.mult).then_inc(v_rq, 1)
                dve.wait_ge(v_rq, g.n + 1)
                vv.tensor_tensor(Q2[:], bank(B4), Q2[:], ALU.add).then_inc(v_ni, 1)

            def dh(g):
                dve.wait_ge(a_nn, g.n + 1)
                vv.tensor_tensor(DH[:], H1T[:, g.slot], Q2[:], ALU.subtract).then_inc(v_dh0, 1)
                dve.wait_ge(a_z, g.n + 1)
                dve.wait_ge(v_dh0, g.n + 1)
                vv.scalar_tensor_tensor(DH[:], TZ[:], 1.0, DH[:], ALU.add, ALU.mult).then_inc(v_dh1, 1)
                dve.wait_ge(v_dh1, g.n + 1)
                vv.scalar_tensor_tensor(DH[:], DH[:], 0.5, Q2[:], ALU.mult, ALU.add).then_inc(v_dh, 1)

            def x2(g):
                dve.wait_ge(pe_gruT, g.n + 1)
                vv.tensor_tensor(X2[:, g.slot % 2], bank(B7), X1[:, g.slot], ALU.add).then_inc(v_x2, 1)

            def bn2(g):
                dve.wait_ge(v_x2, g.n + 1)
                stats(2, g, X2[:, g.slot % 2]).then_inc(v_bn[2], 1)

            def hle(g):
                dve.wait_ge(pe_hl, g.n + 1)
                bias = ROWV[:, ROW_AT["L2_gnn_bl"]:ROW_AT["L2_gnn_bl"] + 3 * D].rearrange("p (w n) -> p w n", w=3)
                vv.tensor_tensor(HLR[:, :, :, 0:D],
                                 PS[:, B1:B4 + 1, 0:3 * D].rearrange("p g (w n) -> p g w n", w=3),
                                 bias.unsqueeze(1).to_broadcast([128, G, 3, D]), ALU.add).then_inc(v_hl, 1)

            def de(g):
                dve.wait_ge(a_sim, g.n + 1)
                vv.tensor_tensor(DE[:], EE[:], ADJT[:, g.slot], ALU.mult).then_inc(v_de, 1)

            def zs(g):
                dve.wait_ge(a_sim, g.n + 1)
                vv.tensor_reduce(ZS[:, g.slot % 2], EE[:], AX_X, ALU.add).then_inc(v_zs, 1)

            def diag(g):
                dve.wait_ge(p_di, g.n + 1)
                vv.tensor_reduce(DG[:, g.slot % 2], DI[:], AX_X, ALU.add).then_inc(v_diag, 1)

            def cc(g):
                p = g.slot % 2
                wide = pair_wide(B6, D + 1)
                dve.wait_ge(pe_ctx, g.n + 1)
                dve.wait_ge(p_hsd, g.n + 1)
                vv.tensor_tensor(DEN[:, 0, p], wide[:, :, D:D + 1].rearrange("p g o -> p (g o)"), DG[:, p],
                                 ALU.add).then_inc(v_den0, 1)
                vv.tensor_tensor(CC[:], wide[:, :, 0:D], HSD[:], ALU.add).then_inc(v_cc, 1)
                dve.wait_ge(v_zs, g.n + 1)
                dve.wait_ge(v_den0, g.n + 1)
                vv.scalar_tensor_tensor(DEN[:, 1, p], ZS[:, p], L2_RENORM_EPS, DEN[:, 0, p], ALU.mult,
                                        ALU.add).then_inc(v_den, 1)

            def bn4(g):
                dve.wait_ge(v_cc, g.n + 1)
                stats(4, g, CC).then_inc(v_bn[4], 1)

            def x3(g):
                dve.wait_ge(p_lnb, g.n + 1)
                vv.scalar_tensor_tensor(X3[:, g.slot % 2], CH[:], 0.0, X2[:, g.slot % 2], ALU.max,
                                        ALU.add).then_inc(v_x3, 1)

            def bn3(g):
                dve.wait_ge(v_x3, g.n + 1)
                stats(3, g, X3[:, g.slot % 2]).then_inc(v_bn[3], 1)

            def gp(g):
                dve.wait_ge(pe_hg, g.n + 1)
                vv.tensor_tensor(GP[:], bank(B2), row("L3_gnn_b_t"), ALU.add).then_inc(v_gp, 1)

            def mix(g):
                dve.wait_ge(a_fh, g.n + 1)
                dve.wait_ge(a_het, g.n + 1)
                vv.tensor_tensor(FH[:], FH[:], HET[:], ALU.subtract).then_inc(v_mix0, 1)
                dve.wait_ge(a_gate, g.n + 1)
                dve.wait_ge(v_mix0, g.n + 1)
                vv.scalar_tensor_tensor(FH[:], GP[:], 1.0, FH[:], ALU.add, ALU.mult).then_inc(v_mix1, 1)
                dve.wait_ge(v_mix1, g.n + 1)
                vv.scalar_tensor_tensor(FH[:], FH[:], 0.5, HET[:], ALU.mult, ALU.add).then_inc(v_mix, 1)

            def out_(g):
                dve.wait_ge(a_ex, g.n + 1)
                dve.wait_ge(p_x3m, g.n + 1)
                vv.scalar_tensor_tensor(EX[:], EX[:], 1.0, X3M[:, g.slot % 2], ALU.min, ALU.add).then_inc(v_out0, 1)
                if g.has(2):
                    dve.wait_ge(out_stored[(g.slot + 2) % 4], (g.turn + (1 if g.slot >= 2 else 0)) * 16)
                dve.wait_ge(v_out0, g.n + 1)
                vv.scalar_tensor_tensor(OUT[:, g.slot % 2], FH[:], 0.0, EX[:], ALU.max, ALU.add).then_inc(v_out, 1)

            def one_step(turn, step):
                a, b, c, d = (group(turn, step, lag) for lag in range(LAGS))
                if a:
                    deg(a)
                if b:
                    c1L(b)
                    msgp(b)
                if a:
                    bn0(a)
                if b:
                    s(b)
                if c:
                    ni(c)
                if d:
                    x3(d)
                    bn3(d)
                if c:
                    dh(c)
                    x2(c)
                    bn2(c)
                if a:
                    x1(a)
                    bn1(a)
                if b:
                    nmL(b)
                if d:
                    gp(d)
                if c:
                    de(c)
                if d:
                    mix(d)
                if c:
                    hle(c)
                    diag(c)
                    zs(c)
                if b:
                    xc(b)
                if c:
                    cc(c)
                    bn4(c)
                if d:
                    out_(d)
                if b:
                    xcL(b)

            schedule(dve, one_step)

        @block.tensor
        def _(pe):
            mm = nc.tensor.matmul

            def mm3(o, weight, hi, lo, start, stop):
                wh, wl = weight
                mm(o, wh, hi, start=start, stop=False)
                mm(o, wh, lo, start=False, stop=False)
                return mm(o, wl, hi, start=False, stop=stop)

            def transposes(b, src):
                for j in range(G):
                    last = nc.tensor.transpose(bank(b)[:, j], src[:, j], ident)
                return last

            def products(b, left, right):
                for j in range(G):
                    last = mm(bank(b)[:, j], left(j), right(j), start=True, stop=True)
                return last

            def conv1(g):
                pe.wait_ge(a_h1H, g.n + 1)
                pe.wait_ge(p_h1L, g.n + 1)
                mm3(PS[:, B5, :], w("conv1", 0), flat(H1H[:, g.slot]), flat(H1L[:, g.slot]), True,
                    True).then_inc(pe_conv1, 1)

            def msg(g):
                wide = pair_wide(B6, D + 3)
                if g.has(2):
                    pe.wait_ge(v_den, g.n - 1)
                pe.wait_ge(a_h1T, g.n + 1)
                for j in range(G):
                    last = mm(wide[:, j], H1T[:, g.slot, j], WMSG[:], start=True, stop=True)
                last.then_inc(pe_msg, 1)

            def gruH(g):
                h = (flat(H1H[:, g.slot]), flat(H1L[:, g.slot]))
                pe.wait_ge(p_h1L, g.n + 1)
                mm3(PS[:, B3, :], w("whh", 2), *h, True, True).then_inc(pe_gruH, 1)
                mm3(PS[:, B1, :], w("whh", 0), *h, True, False)
                mm3(PS[:, B2, :], w("whh", 1), *h, True, False)

            def gruN(g):
                nm = (flat(NMH[:, g.slot % 2]), flat(NML[:, g.slot % 2]))
                pe.wait_ge(a_nmH, g.n + 1)
                pe.wait_ge(v_nmL, g.n + 1)
                mm3(PS[:, B1, :], w("wih", 3), *nm, False, False)
                mm3(PS[:, B2, :], w("wih", 4), *nm, False, False)
                mm3(PS[:, B4, :], w("wih", 5), *nm, True, False).then_inc(pe_gruN, 1)

            def gruX(g):
                xc = (flat(XCH[:]), flat(XCL[:]))
                pe.wait_ge(a_xcH, g.n + 1)
                pe.wait_ge(v_xcL, g.n + 1)
                mm3(PS[:, B1, :], w("wih", 0), *xc, False, True)
                mm3(PS[:, B4, :], w("wih", 2), *xc, False, True)
                mm3(PS[:, B2, :], w("wih", 1), *xc, False, True).then_inc(pe_gruX, 1)

            def adjT(g):
                pe.wait_ge(adj_in[g.slot], (g.turn + 1) * 16)
                transposes(B5, ADJ[:, g.slot % 2]).then_inc(pe_adjT, 1)

            def u0(g):
                pe.wait_ge(a_hp, g.n + 1)
                pe.wait_ge(p_adji, g.n + 1)
                products(B5, lambda j: HP[:, j], lambda j: ADJI[:, j]).then_inc(pe_u0, 1)

            def y0(g):
                pe.wait_ge(a_u0, g.n + 1)
                products(B5, lambda j: UT[:, j], lambda j: W0[:]).then_inc(pe_y0, 1)

            def h1T(g):
                pe.wait_ge(a_xh1, g.n + 1)
                transposes(B5, XH1).then_inc(pe_h1T, 1)

            def sT(g):
                pe.wait_ge(v_slr, g.n + 1)
                for side in (0, 1):
                    for j in range(G):
                        last = nc.tensor.transpose(PS[0:5, B6 + side, j * N:(j + 1) * N], SLR[:, j, side, 0:5], ident)
                last.then_inc(pe_sT, 1)

            def dist(g):
                pe.wait_ge(a_sT, g.n + 1)
                products(B6, lambda j: LRT[0:5, 0, j], lambda j: LRT[0:5, 1, j]).then_inc(pe_dist, 1)

            def nmp(g):
                pe.wait_ge(a_msg, g.n + 1)
                pe.wait_ge(p_at, g.n + 1)
                products(B6, lambda j: MSG[:, j], lambda j: AT[:, j]).then_inc(pe_nmp, 1)

            centre_first = [PAD] + [k for k in range(TAPS) if k != PAD]

            def conv2(g, part):
                o = bank(B0)
                for i in range(part * SHARE, min(TAPS, (part + 1) * SHARE)):
                    off = centre_first[i] - PAD
                    skip = abs(off) // 2 * 2
                    a, n = (skip if off < 0 else 0), N - skip
                    hi = C1H[:, :, a + off + PAD:a + off + PAD + n]
                    lo = C1L[:, :, a + off + PAD:a + off + PAD + n]
                    last = mm3(o[:, :, a:a + n], w("conv2", off + PAD), hi, lo, i == 0, i == TAPS - 1)
                return last

            def cv0(g):
                pe.wait_ge(a_c1H, g.n + 1)
                pe.wait_ge(v_c1L, g.n + 1)
                conv2(g, 0)

            def cv5(g):
                conv2(g, 5).then_inc(pe_conv2, 1)

            def gruT(g):
                if g.has(-1):
                    pe.wait_ge(a_sT, g.n + 2)
                pe.wait_ge(v_dh, g.n + 1)
                transposes(B7, DH).then_inc(pe_gruT, 1)

            def h2T(g):
                pe.wait_ge(a_xh2, g.n + 1)
                transposes(B7, XH2).then_inc(pe_h2T, 1)

            def sim(g):
                pe.wait_ge(a_h2T, g.n + 1)
                products(B7, lambda j: H2T[:, j], lambda j: H2T[:, j]).then_inc(pe_sim, 1)

            def hl(g):
                wh, wl = w("wlsr", 0, 3)
                if g.has(1):
                    pe.wait_ge(a_het, g.n)
                if g.has(1):
                    pe.wait_ge(v_gp, g.n)
                pe.wait_ge(p_h2L, g.n + 1)
                for j in range(G):
                    o = PS[:, B1 + j, 0:3 * D]
                    mm(o, H2H[:, j], wh, start=True, stop=False)
                    mm(o, H2H[:, j], wl, start=False, stop=False)
                    last = mm(o, H2L[:, j], wh, start=False, stop=True)
                last.then_inc(pe_hl, 1)

            def ctx_(g):
                wide = pair_wide(B6, D + 1)
                pe.wait_ge(p_dl, g.n + 1)
                pe.wait_ge(v_hl, g.n + 1)
                for j in range(G):
                    mm(wide[:, j], DL[:, j], HLR[:, j, 0, 0:D + 1], start=True, stop=False)
                    last = mm(wide[:, j], DR[:, j], HLR[:, j, 2, 0:D + 1], start=False, stop=True)
                last.then_inc(pe_ctx, 1)

            def h3T(g):
                pe.wait_ge(a_xh3, g.n + 1)
                transposes(B1, XH3).then_inc(pe_h3T, 1)

            def g3(g):
                pe.wait_ge(a_hn3, g.n + 1)
                products(B2, lambda j: HN[:, j], lambda j: ADJT[:, g.slot, j]).then_inc(pe_g3, 1)

            def fhom(g):
                pe.wait_ge(a_g3, g.n + 1)
                products(B3, lambda j: G3T[:, j], lambda j: THETA[:]).then_inc(pe_fhom, 1)

            def hg(g):
                pe.wait_ge(a_h3T, g.n + 1)
                products(B1, lambda j: H3T[:, j], lambda j: WHET[:, 0:D])
                products(B2, lambda j: H3T[:, j], lambda j: WHET[:, D:2 * D]).then_inc(pe_hg, 1)

            pe.wait_ge(consts_in, 48)
            pe.wait_ge(weights_in, 64)
            pe.wait_ge(piece_lo, len(cuts))

            def one_step(turn, step):
                a, b, c, d = (group(turn, step, lag) for lag in range(LAGS))
                if b:
                    cv0(b)
                if a:
                    adjT(a)
                if b:
                    conv2(b, 1)
                    sT(b)
                    conv2(b, 2)
                    conv2(b, 3)
                if c:
                    gruT(c)
                if b:
                    dist(b)
                if d:
                    g3(d)
                if a:
                    u0(a)
                if d:
                    h3T(d)
                if b:
                    conv2(b, 4)
                if a:
                    y0(a)
                if d:
                    fhom(d)
                if c:
                    h2T(c)
                if b:
                    nmp(b)
                if d:
                    hg(d)
                if c:
                    sim(c)
                    hl(c)
                if a:
                    h1T(a)
                if b:
                    cv5(b)
                if c:
                    ctx_(c)
                if b:
                    gruH(b)
                if a:
                    conv1(a)
                if b:
                    gruN(b)
                if a:
                    msg(a)
                if b:
                    gruX(b)

            schedule(pe, one_step)


def kernel(**inputs):
    import concourse.bacc as bacc
    from concourse.bass_utils import run_bass_kernel_spmd

    def arr(name):
        return np.asarray(inputs[name])

    m, n = np.arange(N)[:, None], np.arange(N)[None, :]
    eye = np.ascontiguousarray(np.stack([m == n, m > n, m < n], axis=1).astype(np.float32))
    bih, bhh = arr("L1_gnn_b_ih").reshape(3, D), arr("L1_gnn_b_hh").reshape(3, D)
    arrays = {
        "x": arr("x"),
        "adj": arr("adj"),
        "eye": eye,
        "rows": np.concatenate([arr(r) for r in ROWS]),
        "cols": np.ascontiguousarray(np.stack(
            [arr("L1_gnn_" + c) for c in COLS[:8]] + [bih[0], bih[1], bih[2], bhh[0], bhh[1], bhh[2]], axis=1)),
        "w0": arr("L0_gnn_W"),
        "conv1T": np.ascontiguousarray(arr("L1_gnn_conv1_w")[:, :, 0].T),
        "conv2T": np.ascontiguousarray(arr("L1_gnn_conv2_w").transpose(1, 2, 0).reshape(D, TAPS * D)),
        "wmsgT": np.ascontiguousarray(np.concatenate([arr("L1_gnn_w_msg"), arr("L1_gnn_w_se")]).T),
        "wihT": np.ascontiguousarray(arr("L1_gnn_w_ih").T.reshape(2, D, 3 * D).transpose(1, 0, 2).reshape(D, 6 * D)),
        "whhT": np.ascontiguousarray(arr("L1_gnn_w_hh").T),
        "wlsrT": np.ascontiguousarray(np.concatenate([arr("L2_gnn_Wl"), arr("L2_gnn_Ws"), arr("L2_gnn_Wr")]).T),
        "whet": np.ascontiguousarray(np.concatenate([arr("L3_gnn_W_h"), arr("L3_gnn_W_t")], axis=1)),
        "theta": arr("L3_gnn_theta"),
    }
    nc = bacc.Bacc("TRN2", target_bir_lowering=False, num_devices=1)
    args, feeds = [], {}
    for name, a in arrays.items():
        feeds[f"in_{name}"] = a
        args.append(nc.dram_tensor(f"in_{name}", a.shape, F32, kind="ExternalInput").ap())
    args.append(nc.dram_tensor("out_0", (B, N, D), F32, kind="ExternalOutput").ap())
    build(nc, *args)
    r = run_bass_kernel_spmd(nc, [feeds], core_ids=[0])
    return r.results[0]["out_0"]
```

```python
from collections import namedtuple
from contextlib import ExitStack

import numpy as np

import concourse.bass as bass
from concourse import mybir

F32 = mybir.dt.float32
F32R = mybir.dt.float32r
ALU = mybir.AluOpType
ACT = mybir.ActivationFunctionType
AX_X = mybir.AxisListType.X

B, N, D = 128, 128, 128
G = 4
GROUPS = B // G
LAGS = 5
PEELED = 2
ROUND = 4
TAPS = 17
EVEN, ODD = TAPS // 2 + 1, TAPS // 2
HALF = N // 2
WIDE = N // 2 + TAPS // 2
SHARE = 3
PAD = TAPS // 2
LN_EPS = 1e-5
L2_LN_EPS = 1e-12
L2_RENORM_EPS = 1e-10
L3_DEG_EPS = 1e-6
BN_EPS = 1e-5

ROWS = ("L0_gnn_b", "L1_gnn_b_msg", "L1_gnn_b_se", "L2_gnn_bl", "L2_gnn_bs", "L2_gnn_br",
        "L2_gnn_ln_w", "L2_gnn_ln_b", "L3_gnn_b_t")
ROW_SIZE = {"L1_gnn_b_se": 3}
ROW_AT = {}
_at = 0
for _name in ROWS:
    ROW_AT[_name] = _at
    _at += ROW_SIZE.get(_name, D)
ROW_TOTAL = _at
SPLIT = {"conv1": 1, "whh": 3, "wih": 6, "whet": 2, "wlsr": 3, "conv2": TAPS}
SPLIT_AT = {}
SPLIT_TOTAL = 0
for _name in SPLIT:
    SPLIT_AT[_name] = SPLIT_TOTAL
    SPLIT_TOTAL += SPLIT[_name]
STAGE = 2 * G
STAGES = -(-SPLIT_TOTAL // STAGE)


def stages_of(name):
    return -(-(SPLIT_AT[name] + SPLIT[name]) // STAGE)


COLS = ("bn1_g", "bn1_b", "bn1_m", "bn1_v", "bn2_g", "bn2_b", "bn2_m", "bn2_v",
        "bih_r", "bih_z", "bih_n", "bhh_r", "bhh_z", "bhh_n")
COL_AT = {n: i for i, n in enumerate(COLS)}

BANKS = {"conv2": 0, "u0": 7, "y0": 3, "cvM": 2, "h1T": 6, "conv1": 5, "msg": 6,
         "sT": 3, "dist": 5, "nmp": 5, "gruT": 4, "h2T": 1, "sim": 2, "ctx": 6, "h3T": 5,
         "g3": 5, "hg": 1, "fhom": 5, "hlA": 3, "hlB": 6, "r": 1, "z": 2, "hn": 3, "in": 4}

class Group(namedtuple("Group", "n slot turn")):
    def has(self, back):
        return not isinstance(self.n, int) or 0 <= self.n - back < GROUPS

    @property
    def first(self):
        return isinstance(self.n, int) and self.n == 0


def group(turn, step, lag):
    s = step - lag
    if isinstance(turn, int) and not 0 <= turn * ROUND + s < GROUPS:
        return None
    return Group(turn * ROUND + s, s % ROUND, turn + s // ROUND)


def build(nc, x, adj, adjT, eye, rows, cols, w0, wmsgT, theta, split_w, out):
    ctx = ExitStack()

    def sb(name, shape, dt=F32):
        return ctx.enter_context(nc.sbuf_tensor(name, [128, *shape], dt))

    def sem(name):
        return ctx.enter_context(nc.semaphore(name))

    with ctx:
        PS = ctx.enter_context(nc.psum_tensor("banks", [128, 8, 512], F32))

        def whole(name):
            return PS[:, BANKS[name], :]

        def bank(name):
            return whole(name).rearrange("p (g n) -> p g n", n=N)

        def pair_wide(name, w):
            b = BANKS[name]
            return PS[:, b:b + 2, :].rearrange("p b (g n) -> p (b g) n", n=256)[:, :, 0:w]

        EYE = sb("EYE", [3, N])
        ROWV = sb("ROWV", [ROW_TOTAL])
        COLV = sb("COLV", [len(COLS)])
        CW = sb("CW", [8])
        CG = sb("CG", [4])
        CT = sb("CT", [8])
        W0 = sb("W0", [D])
        WMSG = sb("WMSG", [D + 3])
        THETA = sb("THETA", [D])
        WHI = sb("WHI", [SPLIT_TOTAL * D], F32R)
        WLO = sb("WLO", [SPLIT_TOTAL * D], F32R)
        MHALF = sb("MHALF", [12])
        EPS = sb("EPS", [8])

        def w(name, c, n=1):
            a = (SPLIT_AT[name] + c) * D
            return WHI[:, a:a + n * D], WLO[:, a:a + n * D]

        X = sb("X", [2, G, D])
        ADJ = sb("ADJ", [2, G, N])
        ADJT = sb("ADJT", [4, G, N])
        ADJI = sb("ADJI", [G, N])
        XB = sb("XB", [G, D])
        DEG = sb("DEG", [4, G])
        ST = [sb(f"ST{k}", [G, 6]) for k in range(5)]
        MV = [sb(f"MV{k}", [2, G, 2]) for k in range(5)]
        NM = [sb(f"NM{k}", [2, G]) for k in range(5)]
        VE = [sb(f"VE{k}", [2, G]) for k in range(5)]
        RS = [sb(f"RS{k}", [2, G]) for k in range(5)]
        NR = [sb(f"NR{k}", [2, G]) for k in range(5)]
        PW = sb("PW", [2, 12])
        ZD = sb("ZD", [G])
        KEEP = sb("KEEP", [2, G])
        SC0, BI0, SC3, BI3 = [sb(n, [2, G]) for n in ("SC0", "BI0", "SC3", "BI3")]
        ONE = sb("ONE", [1])
        DN = sb("DN", [4, 12])
        HP = sb("HP", [G, D])
        UT = sb("UT", [G, N])
        X1 = sb("X1", [4, G, D])
        XH1 = sb("XH1", [G, D])
        H1T = sb("H1T", [4, G, N])
        H1H = sb("H1H", [4, G, N], F32R)
        H1L = sb("H1L", [4, G, N], F32R)
        C1 = sb("C1", [G, N + 2 * PAD])
        CD = sb("CD", [2, G, WIDE])
        SH = sb("SH", [3, G, WIDE], F32R)
        SL = sb("SL", [3, G, WIDE], F32R)
        SUMH = sb("SUMH", [ODD * D], F32R)
        SUML = sb("SUML", [ODD * D], F32R)
        MS = C1[:, :, PAD:PAD + HALF]
        MSG = sb("MSG", [G, D])
        SS = sb("SS", [G, 3])
        SQ = sb("SQ", [G, 4])
        SLR = sb("SLR", [G, 2, 4, 4], F32R)
        LRT = ctx.enter_context(nc.sbuf_tensor("LRT", [16, 2, G, N], F32R))
        EA = sb("EA", [G, N])
        AT = sb("AT", [G, N])
        NMH = sb("NMH", [G, N], F32R)
        NML = sb("NML", [G, N], F32R)
        XCP = sb("XCP", [G, N])
        XCH = sb("XCH", [G, N], F32R)
        XCL = sb("XCL", [G, N], F32R)
        TR = sb("TR", [G, N])
        TZ = sb("TZ", [G, N])
        Q2 = sb("Q2", [G, N])
        DH = sb("DH", [G, N])
        X2 = sb("X2", [2, G, D])
        XH2 = sb("XH2", [G, D])
        H2T = sb("H2T", [G, N])
        H2H = sb("H2H", [G, N], F32R)
        H2L = sb("H2L", [G, N], F32R)
        EE = sb("EE", [G, N])
        DE = sb("DE", [G, N])
        DL = sb("DL", [G, N])
        DR = sb("DR", [G, N])
        ZS = sb("ZS", [2, G])
        DG = sb("DG", [2, G])
        HLR = sb("HLR", [G, 3, D + 4])
        HSD = sb("HSD", [G, D])
        DEN = sb("DEN", [2, 2, G])
        CH = sb("CH", [G, D])
        X3 = sb("X3", [2, G, D])
        XH3 = sb("XH3", [G, D])
        HN = sb("HN", [G, D])
        H3H = sb("H3H", [G, N], F32R)
        H3L = sb("H3L", [G, N], F32R)
        G3T = sb("G3T", [G, N])
        X3M = sb("X3M", [2, G, D])
        HET = sb("HET", [G, D])
        FH = sb("FH", [G, D])
        GP = sb("GP", [G, D])
        EX = sb("EX", [G, D])
        OUT = sb("OUT", [2, G, D])
        staging = [t.rearrange("p s g d -> p (s g d)") for t in (X2, X3, X3M, OUT)]

        x_in = [sem(f"x_in{s}") for s in range(4)]
        adj_in = [sem(f"adj_in{s}") for s in range(4)]
        adjT_in = [sem(f"adjT_in{s}") for s in range(4)]
        out_stored = [sem(f"out_stored{s}") for s in range(4)]
        consts_in = sem("consts_in")
        weights_in = sem("weights_in")
        stage_in = [sem(f"stage_in{k}") for k in range(STAGES)]
        split_hi = sem("split_hi")
        split_lo = sem("split_lo")
        consts_pool = sem("consts_pool")
        consts_ready = sem("consts_ready")
        (pe_conv1, pe_msg, pe_gruH, pe_gruN, pe_gruX, pe_h3T, pe_g3, pe_sT, pe_u0, pe_hg, pe_fhom,
         pe_dist, pe_y0, pe_gruT, pe_nmp, pe_h2T, pe_h1T, pe_sim, pe_hlA, pe_hlB, pe_conv2, pe_m, pe_ctx) = [
            sem("pe_" + s) for s in
            "conv1 msg gruH gruN gruX h3T g3 sT u0 hg fhom dist y0 gruT nmp h2T h1T sim hlA hlB conv2 m ctx".split()]
        (a_hp, a_u0, a_yd, a_xh1, a_h1T, a_h1H, a_c1, a_c1H, a_m, a_msg, a_sT, a_exp, a_nmH, a_xcH, a_r,
         a_q2, a_z, a_nn, a_xh2, a_h2T, a_h2H, a_sim, a_ch, a_xh3, a_hn3, a_h3H, a_g3, a_fh, a_het, a_gate,
         a_ex) = [sem("a_" + s) for s in
                  ("hp u0 yd xh1 h1T h1H c1 c1H m msg sT exp nmH xcH r q2 z nn xh2 h2T h2H sim ch xh3 hn3 "
                   "h3H g3 fh het gate ex").split()]
        (v_sum, v_zd, v_deg, v_x1, v_c1L, v_msgp, v_s, v_slr, v_nmL, v_xm, v_xc, v_xcL, v_rq, v_ni,
         v_dh01, v_dh, v_x2, v_hleA, v_hleB, v_de, v_diag, v_cc, v_den0, v_den, v_x3, v_h3L, v_gp, v_mix01,
         v_mix, v_out0, v_out) = [sem("v_" + s) for s in
                                  ("sum zd deg x1 c1L msgp s slr nmL xm xc xcL rq ni dh01 dh x2 hleA hleB de "
                                   "diag cc den0 den x3 h3L gp mix01 mix out0 out").split()]
        v_st, v_nm, v_bn = [[sem(f"v_{s}{k}") for k in range(5)] for s in ("st", "nm", "bn")]
        p_ve, p_pw, p_rs = [[sem(f"p_{s}{k}") for k in range(5)] for s in ("ve", "pw", "rs")]
        (p_keep, p_sc0, p_sc3, p_adji, p_cd, p_xb, p_h1L, p_at, p_h2L, p_dl, p_di, p_hsd, p_d23, p_lnw, p_lnb,
         p_x3m) = [sem("p_" + s) for s in
                   "keep sc0 sc3 adji cd xb h1L at h2L dl di hsd d23 lnw lnb x3m".split()]

        def row(name):
            n = ROW_SIZE.get(name, D)
            return ROWV[:, ROW_AT[name]:ROW_AT[name] + n].unsqueeze(1).to_broadcast([128, G, n])

        def per_graph(v):
            return v.unsqueeze(2).to_broadcast([128, G, D])

        def mask(k):
            return EYE[:, k, :].unsqueeze(1).to_broadcast([128, G, N])

        def flat(t):
            return t.rearrange("p g n -> p (g n)")

        def parity(t, odd):
            return t.rearrange("p g (i t) -> p g i t", t=2)[:, :, :, odd]

        ident = EYE[:, 0, :]
        x_d = x.rearrange("(s g) n d -> s n g d", g=G)
        adjT_d = adjT.rearrange("(s g) m n -> s m g n", g=G)
        adj_d = adj.rearrange("(s g) n m -> s n g m", g=G)
        out_d = out.rearrange("(s g) n d -> s n g d", g=G)

        def schedule(engine, one_step):
            for turn in range(PEELED):
                for step in range(ROUND):
                    one_step(turn, step)
            with engine.Fori(PEELED, GROUPS // ROUND) as turn:
                for step in range(ROUND):
                    one_step(turn, step)
            for step in range(LAGS - 1):
                one_step(GROUPS // ROUND, step)

        block = ctx.enter_context(nc.Block())

        @block.sync
        def _(sp):
            sp.dma_start(EYE[:], eye).then_inc(consts_in, 16)
            sp.dma_start(COLV[:], cols).then_inc(consts_in, 16)
            sp.dma_start(ROWV[:], rows.partition_broadcast(128)).then_inc(consts_in, 16)

            def load(g):
                if g.has(2):
                    sp.wait_ge(p_xb, g.n - 1)
                    sp.wait_ge(a_hp, g.n - 1)
                sp.dma_start(X[:, g.slot % 2], x_d[g.n]).then_inc(x_in[g.slot], 16)
                if g.has(2):
                    sp.wait_ge(v_sum, g.n - 1)
                sp.dma_start(ADJ[:, g.slot % 2], adj_d[g.n]).then_inc(adj_in[g.slot], 16)
                if g.has(4):
                    sp.wait_ge(pe_g3, g.n - 3)
                sp.dma_start(ADJT[:, g.slot], adjT_d[g.n]).then_inc(adjT_in[g.slot], 16)

            def store(g):
                sp.wait_ge(v_out, g.n + 1)
                sp.dma_start(out_d[g.n], OUT[:, g.slot % 2]).then_inc(out_stored[g.slot], 16)

            def weights():
                sp.dma_start(W0[:], w0).then_inc(weights_in, 16)
                sp.dma_start(WMSG[:], wmsgT).then_inc(weights_in, 16)
                sp.dma_start(THETA[:], theta).then_inc(weights_in, 16)

            def split_weights():
                for k in range(STAGES):
                    a, n = k * STAGE * D, min(STAGE, SPLIT_TOTAL - k * STAGE) * D
                    sp.dma_start(staging[k][:, 0:n], split_w[:, a:a + n]).then_inc(stage_in[k], 16)

            def one_step(turn, step):
                g, d = group(turn, step, -1), group(turn, step, LAGS - 1)
                if isinstance(turn, int) and turn == 0 and step == 0:
                    load(group(0, 0, 0))
                    weights()
                    split_weights()
                    load(group(0, 1, 0))
                elif g is not None and (not isinstance(turn, int) or turn * ROUND + step + 1 < GROUPS):
                    load(g)
                if d is not None:
                    store(d)

            for turn in range(PEELED):
                for step in range(ROUND):
                    one_step(turn, step)
            with sp.Fori(PEELED, GROUPS // ROUND - 1) as turn:
                for step in range(ROUND):
                    one_step(turn, step)
            for step in range(ROUND):
                one_step(GROUPS // ROUND - 1, step)
            for step in range(LAGS - 1):
                one_step(GROUPS // ROUND, step)
            for s in range(4):
                sp.wait_ge(out_stored[s], 16 * (GROUPS // 4))

        @block.gpsimd
        def _(pool):
            pp = nc.gpsimd
            links = [0]

            def small(ins):
                links[0] += 1
                ins.then_inc(consts_pool, 1)
                pool.wait_ge(consts_pool, links[0])

            def col(n):
                return COLV[:, COL_AT[n]:COL_AT[n] + 1]

            small(pp.memset(MHALF[:], -0.5))
            small(pp.memset(ONE[:], 1.0))
            small(pp.memset(EPS[:, 0:4], LN_EPS))
            small(pp.memset(EPS[:, 4:8], L2_LN_EPS))
            pool.wait_ge(consts_in, 48)

            def constants():
                small(pp.memset(HLR[:], 1.0))
                small(pp.memset(SLR[:].bitcast(F32), 1.0))
                small(pp.memset(C1[:], 0.0))
                small(pp.memset(CD[:], 0.0))
                for k in (0, 1):
                    bn = f"bn{k + 1}_"
                    small(pp.tensor_scalar(CT[:, 0:1], col(bn + "v"), BN_EPS, None, ALU.add))
                    small(pp.tensor_tensor(CT[:, 1:2], CT[:, 0:1], MHALF[:, 0:1], ALU.pow))
                    small(pp.tensor_tensor(CW[:, 2 * k:2 * k + 1], CT[:, 1:2], col(bn + "g"), ALU.mult))
                    small(pp.tensor_tensor(CT[:, 2:3], CW[:, 2 * k:2 * k + 1], col(bn + "m"), ALU.mult))
                    small(pp.tensor_tensor(CW[:, 2 * k + 1:2 * k + 2], col(bn + "b"), CT[:, 2:3], ALU.subtract))
                for k, gate in enumerate("rz"):
                    small(pp.tensor_tensor(CT[:, 3:4], col("bih_" + gate), col("bhh_" + gate), ALU.add))
                    small(pp.tensor_scalar(CG[:, k:k + 1], CT[:, 3:4], 0.5, None, ALU.mult))
                small(pp.tensor_scalar(CG[:, 2:3], col("bhh_n"), 0.5, None, ALU.mult))
                pp.tensor_copy(CG[:, 3:4], col("bih_n")).then_inc(consts_ready, 1)

            def pw0(g):
                s, p = g.slot, g.slot % 2
                if g.has(4):
                    pool.wait_ge(a_fh, g.n - 3)
                pool.wait_ge(v_bn[0], g.n + 1)
                pp.tensor_tensor(PW[:, p, 0:4], MV[0][:, p, :, 1], EPS[:, 0:4], ALU.add).then_inc(p_ve[0], 1)
                pool.wait_ge(v_deg, g.n + 1)
                pool.wait_ge(p_ve[0], g.n + 1)
                pp.tensor_tensor(DN[:, s], PW[:, p], MHALF[:], ALU.pow).then_inc(p_pw[0], 1)
                pool.wait_ge(p_pw[0], g.n + 1)
                pp.tensor_tensor(DN[:, s, 4:8], DN[:, s, 4:8], KEEP[:, p], ALU.mult).then_inc(p_keep, 1)
                pool.wait_ge(p_keep, g.n + 1)
                pp.tensor_tensor(SC0[:, p], DN[:, s, 0:4], DN[:, s, 4:8], ALU.mult).then_inc(p_sc0, 1)
                pool.wait_ge(p_sc0, g.n + 1)
                pp.tensor_tensor(BI0[:, p], NM[0][:, p], SC0[:, p], ALU.mult).then_inc(p_rs[0], 1)

            def rstd(k, g):
                p = g.slot % 2
                pool.wait_ge(v_bn[k], g.n + 1)
                pp.tensor_tensor(VE[k][:, p], MV[k][:, p, :, 1], EPS[:, 0:4], ALU.add).then_inc(p_ve[k], 1)
                pool.wait_ge(p_ve[k], g.n + 1)
                pp.tensor_tensor(RS[k][:, p], VE[k][:, p], MHALF[:, 0:4], ALU.pow).then_inc(p_pw[k], 1)
                pool.wait_ge(p_pw[k], g.n + 1)
                return pp.tensor_tensor(NR[k][:, p], NM[k][:, p], RS[k][:, p], ALU.mult)

            def rs1(g):
                if g.first:
                    constants()
                rstd(1, g).then_inc(p_rs[1], 1)

            def rs2(g):
                rstd(2, g).then_inc(p_rs[2], 1)

            def rs3(g):
                p = g.slot % 2
                rstd(3, g)
                pp.tensor_tensor(SC3[:, p], RS[3][:, p], DN[:, g.slot, 8:12], ALU.mult).then_inc(p_sc3, 1)
                pool.wait_ge(p_sc3, g.n + 1)
                pp.tensor_tensor(BI3[:, p], NM[3][:, p], SC3[:, p], ALU.mult).then_inc(p_rs[3], 1)

            def rs4(g):
                p = g.slot % 2
                pool.wait_ge(v_den, g.n + 1)
                pp.tensor_tensor(DEN[:, 0, p], DEN[:, 1, p], DEN[:, 1, p], ALU.mult).then_inc(p_d23, 1)
                pool.wait_ge(p_d23, g.n * 2 + 1)
                pp.tensor_tensor(VE[4][:, p], DEN[:, 0, p], EPS[:, 4:8], ALU.mult).then_inc(p_d23, 1)
                pool.wait_ge(p_d23, g.n * 2 + 2)
                pool.wait_ge(v_bn[4], g.n + 1)
                pp.tensor_tensor(DEN[:, 0, p], VE[4][:, p], MV[4][:, p, :, 1], ALU.add).then_inc(p_ve[4], 1)
                pool.wait_ge(p_ve[4], g.n + 1)
                pp.tensor_tensor(RS[4][:, p], DEN[:, 0, p], MHALF[:, 0:4], ALU.pow).then_inc(p_pw[4], 1)
                pool.wait_ge(p_pw[4], g.n + 1)
                pp.tensor_tensor(NR[4][:, p], NM[4][:, p], RS[4][:, p], ALU.mult).then_inc(p_rs[4], 1)

            def adji(g):
                pool.wait_ge(adjT_in[g.slot], (g.turn + 1) * 16)
                pp.tensor_tensor(ADJI[:], ADJT[:, g.slot], mask(0), ALU.add).then_inc(p_adji, 1)

            def cd(g):
                even, odd = parity(C1, 0), parity(C1, 1)
                pool.wait_ge(a_c1, g.n + 1)
                pp.tensor_tensor(CD[:, 0], even, odd, ALU.subtract)
                pp.tensor_tensor(CD[:, 1, :, 0:WIDE - 1], even[:, :, 1:WIDE], odd[:, :, 0:WIDE - 1],
                                 ALU.subtract).then_inc(p_cd, 1)

            def xb(g):
                pool.wait_ge(x_in[g.slot], (g.turn + 1) * 16)
                pp.tensor_tensor(XB[:], X[:, g.slot % 2], row("L0_gnn_b"), ALU.add).then_inc(p_xb, 1)

            def h1L(g):
                pool.wait_ge(a_h1T, g.n + 1)
                pool.wait_ge(a_h1H, g.n + 1)
                pp.tensor_tensor(H1L[:, g.slot], H1T[:, g.slot], H1H[:, g.slot].bitcast(F32),
                                 ALU.subtract).then_inc(p_h1L, 1)

            def at(g):
                pool.wait_ge(a_exp, g.n + 1)
                pp.tensor_tensor(AT[:], EA[:], ADJT[:, g.slot], ALU.mult).then_inc(p_at, 1)

            def h2L(g):
                pool.wait_ge(a_h2T, g.n + 1)
                pool.wait_ge(a_h2H, g.n + 1)
                pp.tensor_tensor(H2L[:], H2T[:], H2H[:].bitcast(F32), ALU.subtract).then_inc(p_h2L, 1)

            def dl(g):
                pool.wait_ge(v_de, g.n + 1)
                pp.tensor_tensor(DL[:], DE[:], mask(1), ALU.mult)
                pp.tensor_tensor(DR[:], DE[:], mask(2), ALU.mult).then_inc(p_dl, 1)

            def di(g):
                pool.wait_ge(v_de, g.n + 1)
                pp.tensor_tensor(EE[:], DE[:], mask(0), ALU.mult).then_inc(p_di, 1)

            def hsd(g):
                pool.wait_ge(v_diag, g.n + 1)
                pool.wait_ge(v_hleA, g.n + 1)
                pool.wait_ge(v_hleB, g.n + 1)
                pp.tensor_tensor(HSD[:], HLR[:, :, 1, 0:D], per_graph(DG[:, g.slot % 2]),
                                 ALU.mult).then_inc(p_hsd, 1)

            def lnw(g):
                pool.wait_ge(a_ch, g.n + 1)
                pp.tensor_tensor(CH[:], CH[:], row("L2_gnn_ln_w"), ALU.mult).then_inc(p_lnw, 1)

            def lnb(g):
                pool.wait_ge(p_lnw, g.n + 1)
                pp.tensor_tensor(CH[:], CH[:], row("L2_gnn_ln_b"), ALU.add).then_inc(p_lnb, 1)

            def x3m(g):
                pool.wait_ge(v_x3, g.n + 1)
                pp.tensor_tensor(X3M[:, g.slot % 2], X3[:, g.slot % 2],
                                 ONE[:].unsqueeze(2).to_broadcast([128, G, D]), ALU.subtract).then_inc(p_x3m, 1)

            def one_step(turn, step):
                a, b, c, d, e = (group(turn, step, lag) for lag in range(LAGS))
                if a:
                    adji(a)
                    pw0(a)
                if d:
                    lnw(d)
                if c:
                    rs2(c)
                if b:
                    at(b)
                if d:
                    lnb(d)
                if a:
                    xb(a)
                if c:
                    h2L(c)
                if d:
                    rs3(d)
                if a:
                    rs1(a)
                if c:
                    di(c)
                    dl(c)
                if a:
                    h1L(a)
                if c:
                    hsd(c)
                if d:
                    x3m(d)
                if a:
                    cd(a)
                if c:
                    rs4(c)

            schedule(pool, one_step)

        @block.scalar
        def _(act):
            aa = nc.scalar.activation

            def high_parts(first, last):
                for k in range(first, last):
                    a, n = k * STAGE * D, min(STAGE, SPLIT_TOTAL - k * STAGE) * D
                    act.wait_ge(stage_in[k], 16)
                    aa(WHI[:, a:a + n], staging[k][:, 0:n], ACT.Copy).then_inc(split_hi, 1)

            def sums_high_parts():
                for k, t in enumerate((DL, DR)):
                    act.wait_ge(split_lo, STAGES + k + 1)
                    aa(SUMH[:, k * 4 * D:(k + 1) * 4 * D], flat(t[:]), ACT.Copy).then_inc(split_hi, 1)

            def affine(dst, src, scale, bias, func):
                for j in range(G):
                    last = aa(dst[:, j], src[:, j], func, scale=scale[:, j:j + 1], bias=bias[:, j:j + 1])
                return last

            def scaled(dst, src, scale):
                for j in range(G):
                    last = aa(dst[:, j], src[:, j], ACT.Copy, scale=scale[:, j:j + 1])
                return last

            def hp(g):
                p = g.slot % 2
                if g.first:
                    high_parts(0, 2)
                act.wait_ge(p_rs[0], g.n + 1)
                affine(HP, X[:, p], SC0[:, p], BI0[:, p], ACT.Relu).then_inc(a_hp, 1)
                if g.first:
                    high_parts(2, STAGES)

            def u0e(g):
                act.wait_ge(pe_u0, g.n + 1)
                aa(UT[:], bank("u0"), ACT.Copy).then_inc(a_u0, 1)

            def yd(g):
                act.wait_ge(pe_y0, g.n + 1)
                act.wait_ge(p_rs[0], g.n + 1)
                scaled(X1[:, g.slot], bank("y0"), DN[:, g.slot, 4:8]).then_inc(a_yd, 1)

            def xh1(g):
                p = g.slot % 2
                act.wait_ge(p_rs[1], g.n + 1)
                affine(XH1, X1[:, g.slot], RS[1][:, p], NR[1][:, p], ACT.Relu).then_inc(a_xh1, 1)

            def h1Te(g):
                act.wait_ge(pe_h1T, g.n + 1)
                aa(H1T[:, g.slot], bank("h1T"), ACT.Copy).then_inc(a_h1T, 1)

            def h1H(g):
                act.wait_ge(pe_h1T, g.n + 1)
                aa(H1H[:, g.slot], bank("h1T"), ACT.Copy).then_inc(a_h1H, 1)

            def c1(g):
                if g.first:
                    sums_high_parts()
                    act.wait_ge(consts_ready, 1)
                act.wait_ge(pe_conv1, g.n + 1)
                aa(C1[:, :, PAD:PAD + N], bank("conv1"), ACT.Relu, scale=CW[:, 0:1], bias=CW[:, 1:2]).then_inc(a_c1, 1)

            def c1H(g):
                act.wait_ge(a_c1, g.n + 1)
                aa(SH[:, 0], parity(C1, 1), ACT.Copy)
                act.wait_ge(p_cd, g.n + 1)
                aa(SH[:, 1:3], CD[:], ACT.Copy).then_inc(a_c1H, 1)

            def mE(g):
                act.wait_ge(pe_m, g.n + 1)
                aa(MS, whole("cvM")[:, 0:G * HALF].rearrange("p (g i) -> p g i", g=G), ACT.Identity,
                   scale=CW[:, 2:3], bias=CW[:, 3:4]).then_inc(a_m, 1)

            def msgr(g):
                act.wait_ge(v_msgp, g.n + 1)
                aa(MSG[:], MSG[:], ACT.Relu).then_inc(a_msg, 1)

            def sTe(g):
                act.wait_ge(pe_sT, g.n + 1)
                aa(LRT[:].rearrange("p l g n -> p l (g n)"), PS[0:16, BANKS["sT"]:BANKS["sT"] + 2, :], ACT.Copy).then_inc(a_sT, 1)

            def exp(g):
                act.wait_ge(pe_dist, g.n + 1)
                aa(EA[:], bank("dist"), ACT.Exp).then_inc(a_exp, 1)

            def nmH(g):
                act.wait_ge(pe_nmp, g.n + 1)
                aa(NMH[:], bank("nmp"), ACT.Copy).then_inc(a_nmH, 1)

            def xcH(g):
                act.wait_ge(v_xc, g.n + 1)
                aa(XCH[:], XCP[:], ACT.Relu).then_inc(a_xcH, 1)

            def q2(g):
                if g.first:
                    act.wait_ge(consts_ready, 1)
                act.wait_ge(pe_gruH, g.n + 1)
                aa(Q2[:], bank("hn"), ACT.Identity, scale=0.5, bias=CG[:, 2:3]).then_inc(a_q2, 1)

            def r(g):
                act.wait_ge(pe_gruX, g.n + 1)
                aa(TR[:], bank("r"), ACT.Tanh, scale=0.5, bias=CG[:, 0:1]).then_inc(a_r, 1)

            def z(g):
                act.wait_ge(pe_gruX, g.n + 1)
                aa(TZ[:], bank("z"), ACT.Tanh, scale=0.5, bias=CG[:, 1:2]).then_inc(a_z, 1)

            def nn(g):
                act.wait_ge(v_ni, g.n + 1)
                aa(Q2[:], Q2[:], ACT.Tanh, bias=CG[:, 3:4]).then_inc(a_nn, 1)

            def xh2(g):
                p = g.slot % 2
                act.wait_ge(p_rs[2], g.n + 1)
                affine(XH2, X2[:, p], RS[2][:, p], NR[2][:, p], ACT.Relu).then_inc(a_xh2, 1)

            def h2Te(g):
                act.wait_ge(pe_h2T, g.n + 1)
                aa(H2T[:], bank("h2T"), ACT.Copy).then_inc(a_h2T, 1)

            def h2H(g):
                act.wait_ge(pe_h2T, g.n + 1)
                aa(H2H[:], bank("h2T"), ACT.Copy).then_inc(a_h2H, 1)

            def simE(g):
                act.wait_ge(pe_sim, g.n + 1)
                for j in range(G):
                    last = aa(EE[:, j], bank("sim")[:, j], ACT.Exp, scale=float(D) ** -0.5,
                              accum_out=ZS[:, g.slot % 2, j:j + 1])
                last.then_inc(a_sim, 1)

            def ch(g):
                p = g.slot % 2
                act.wait_ge(p_rs[4], g.n + 1)
                affine(CH, HSD, RS[4][:, p], NR[4][:, p], ACT.Identity).then_inc(a_ch, 1)

            def xh3(g):
                p = g.slot % 2
                act.wait_ge(p_rs[3], g.n + 1)
                affine(XH3, X3[:, p], RS[3][:, p], NR[3][:, p], ACT.Relu).then_inc(a_xh3, 1)

            def hn3(g):
                p = g.slot % 2
                act.wait_ge(p_rs[3], g.n + 1)
                affine(HN, X3[:, p], SC3[:, p], BI3[:, p], ACT.Relu).then_inc(a_hn3, 1)

            def h3H(g):
                act.wait_ge(pe_h3T, g.n + 1)
                aa(H3H[:], bank("h3T"), ACT.Copy).then_inc(a_h3H, 1)

            def g3e(g):
                act.wait_ge(pe_g3, g.n + 1)
                aa(G3T[:], bank("g3"), ACT.Copy).then_inc(a_g3, 1)

            def fh(g):
                act.wait_ge(pe_fhom, g.n + 1)
                scaled(FH, bank("fhom"), DN[:, g.slot, 8:12]).then_inc(a_fh, 1)

            def hete(g):
                act.wait_ge(pe_hg, g.n + 1)
                aa(HET[:], pair_wide("hg", D), ACT.Copy).then_inc(a_het, 1)

            def gate(g):
                act.wait_ge(v_gp, g.n + 1)
                aa(GP[:], GP[:], ACT.Tanh, scale=0.5).then_inc(a_gate, 1)

            def ex(g):
                act.wait_ge(v_mix, g.n + 1)
                aa(EX[:], FH[:], ACT.Exp).then_inc(a_ex, 1)

            def one_step(turn, step):
                a, b, c, d, e = (group(turn, step, lag) for lag in range(LAGS))
                if c:
                    nmH(c)
                if e:
                    xh3(e)
                if b:
                    xh1(b)
                if e:
                    hn3(e)
                if b:
                    h1H(b)
                    h1Te(b)
                if e:
                    h3H(e)
                if c:
                    xcH(c)
                if b:
                    c1(b)
                if c:
                    q2(c)
                    r(c)
                if e:
                    g3e(e)
                if c:
                    z(c)
                if b:
                    c1H(b)
                if c:
                    nn(c)
                if e:
                    fh(e)
                    hete(e)
                if b:
                    sTe(b)
                if d:
                    ch(d)
                if e:
                    gate(e)
                if b:
                    exp(b)
                if a:
                    hp(a)
                if b:
                    msgr(b)
                    mE(b)
                if c:
                    xh2(c)
                if a:
                    u0e(a)
                if c:
                    h2Te(c)
                    h2H(c)
                if a:
                    yd(a)
                if c:
                    simE(c)
                if e:
                    ex(e)

            schedule(act, one_step)

        @block.vector
        def _(dve):
            vv = nc.vector

            def low_parts():
                for k in range(STAGES):
                    a, n = k * STAGE * D, min(STAGE, SPLIT_TOTAL - k * STAGE) * D
                    dve.wait_ge(split_hi, k + 1)
                    dve.wait_ge(stage_in[k], 16)
                    vv.tensor_tensor(WLO[:, a:a + n], staging[k][:, 0:n], WHI[:, a:a + n].bitcast(F32),
                                     ALU.subtract).then_inc(split_lo, 1)

            def tap_sums():
                for k, t in enumerate((DL, DR)):
                    taps = staging[2 + k].rearrange("p (j t d) -> p j t d", t=2, d=D)
                    dve.wait_ge(stage_in[2 + k], 16)
                    vv.tensor_tensor(t[:], taps[:, :, 0], taps[:, :, 1], ALU.add).then_inc(split_lo, 1)

            def sums_low_parts():
                for k, t in enumerate((DL, DR)):
                    dve.wait_ge(split_hi, STAGES + k + 1)
                    part = slice(k * 4 * D, (k + 1) * 4 * D)
                    vv.tensor_tensor(SUML[:, part], flat(t[:]), SUMH[:, part].bitcast(F32),
                                     ALU.subtract).then_inc(split_lo, 1)

            def stats(k, g, src):
                p = g.slot % 2
                for j in range(G):
                    last = vv.bn_stats(ST[k][:, j], src[:, j])
                last.then_inc(v_st[k], 1)
                dve.wait_ge(v_st[k], g.n + 1)
                vv.tensor_scalar(NM[k][:, p], ST[k][:, :, 1], -0.5, None, ALU.mult).then_inc(v_nm[k], 1)
                for j in range(G):
                    vv.bn_aggr(MV[k][:, p, j], ST[k][:, j])
                dve.wait_ge(v_nm[k], g.n + 1)
                return vv.scalar_tensor_tensor(NM[k][:, p], ST[k][:, :, 4], -0.5, NM[k][:, p], ALU.mult, ALU.add)

            def deg(g):
                p = g.slot % 2
                sums = DEG[:, g.slot]
                dve.wait_ge(adj_in[g.slot], (g.turn + 1) * 16)
                vv.tensor_reduce(sums, ADJ[:, p], AX_X, ALU.add).then_inc(v_sum, 1)
                dve.wait_ge(v_sum, g.n + 1)
                vv.tensor_scalar(ZD[:], sums, 1.0, 0.0, ALU.add, ALU.is_equal).then_inc(v_zd, 1)
                vv.tensor_scalar(KEEP[:, p], sums, 1.0, 0.0, ALU.add, ALU.not_equal)
                vv.tensor_scalar(PW[:, p, 8:12], sums, L3_DEG_EPS, None, ALU.add)
                dve.wait_ge(v_zd, g.n + 1)
                vv.scalar_tensor_tensor(PW[:, p, 4:8], sums, 1.0, ZD[:], ALU.add, ALU.add).then_inc(v_deg, 1)

            def bn0(g):
                dve.wait_ge(x_in[g.slot], (g.turn + 1) * 16)
                stats(0, g, X[:, g.slot % 2]).then_inc(v_bn[0], 1)

            def x1(g):
                s = g.slot
                if g.first:
                    low_parts()
                    tap_sums()
                dve.wait_ge(a_yd, g.n + 1)
                dve.wait_ge(p_xb, g.n + 1)
                vv.tensor_tensor(X1[:, s], X1[:, s], XB[:], ALU.add).then_inc(v_x1, 1)

            def bn1(g):
                dve.wait_ge(v_x1, g.n + 1)
                stats(1, g, X1[:, g.slot]).then_inc(v_bn[1], 1)

            def c1L(g):
                if g.first:
                    sums_low_parts()
                dve.wait_ge(a_c1H, g.n + 1)
                vv.tensor_tensor(SL[:, 0], parity(C1, 1), SH[:, 0].bitcast(F32), ALU.subtract)
                vv.tensor_tensor(SL[:, 1:3], CD[:], SH[:, 1:3].bitcast(F32), ALU.subtract).then_inc(v_c1L, 1)

            def msgp(g):
                dve.wait_ge(pe_msg, g.n + 1)
                vv.tensor_tensor(MSG[:], pair_wide("msg", D + 3)[:, :, 0:D], row("L1_gnn_b_msg"),
                                 ALU.add).then_inc(v_msgp, 1)

            def s(g):
                left, right = SLR[:, :, 0].bitcast(F32), SLR[:, :, 1].bitcast(F32)
                if g.first:
                    dve.wait_ge(consts_ready, 1)
                dve.wait_ge(pe_msg, g.n + 1)
                vv.tensor_tensor(SQ[:, :, 0:3], pair_wide("msg", D + 3)[:, :, D:D + 3], row("L1_gnn_b_se"),
                                 ALU.add).then_inc(v_s, 1)
                dve.wait_ge(v_s, g.n * 5 + 1)
                vv.tensor_tensor(SS[:], SQ[:, :, 0:3], SQ[:, :, 0:3], ALU.mult).then_inc(v_s, 1)
                dve.wait_ge(v_s, g.n * 5 + 2)
                vv.tensor_reduce(SQ[:, :, 3:4], SS[:], AX_X, ALU.add, negate=True).then_inc(v_s, 1)
                dve.wait_ge(v_s, g.n * 5 + 3)
                vv.tensor_copy(SLR[:, :, 1, 0], SQ[:]).then_inc(v_s, 1)
                dve.wait_ge(v_s, g.n * 5 + 4)
                vv.tensor_tensor(SLR[:, :, 1, 1], SQ[:], right[:, :, 0], ALU.subtract).then_inc(v_s, 1)
                vv.tensor_scalar(SLR[:, :, 0, 0, 0:3], right[:, :, 0, 0:3], 2.0, None, ALU.mult)
                vv.tensor_scalar(SLR[:, :, 0, 1, 0:3], right[:, :, 0, 0:3], 2.0, None, ALU.mult)
                dve.wait_ge(v_s, g.n * 5 + 5)
                vv.tensor_copy(SLR[:, :, 1, 2:4, 0:3], right[:, :, 0:2, 0:3])
                vv.tensor_copy(SLR[:, :, 0, 2:4, 3:4], right[:, :, 0:2, 3:4])
                vv.tensor_scalar(SLR[:, :, 0, 2, 0:3], right[:, :, 1, 0:3], 2.0, None, ALU.mult)
                vv.tensor_scalar(SLR[:, :, 0, 3, 0:3], right[:, :, 1, 0:3], 2.0, None,
                                 ALU.mult).then_inc(v_slr, 1)

            def nmL(g):
                dve.wait_ge(a_nmH, g.n + 1)
                vv.tensor_tensor(NML[:], bank("nmp"), NMH[:].bitcast(F32),
                                 ALU.subtract).then_inc(v_nmL, 1)

            def xm(g):
                dve.wait_ge(a_m, g.n + 1)
                vv.tensor_tensor(XCP[:].rearrange("p g (i t) -> p g i t", t=2),
                                 H1T[:, g.slot].rearrange("p g (i t) -> p g i t", t=2),
                                 MS.unsqueeze(3).to_broadcast([128, G, HALF, 2]), ALU.add).then_inc(v_xm, 1)

            def xc(g):
                dve.wait_ge(pe_conv2, g.n + 1)
                dve.wait_ge(v_xm, g.n + 1)
                x = XCP[:].rearrange("p g (i t) -> p t g i", t=2)
                parts = whole("conv2").rearrange("p (t g i) -> p t g i", t=2, g=G)
                vv.scalar_tensor_tensor(x[:, 0], parts[:, 0], CW[:, 2:3], x[:, 0], ALU.mult, ALU.add)
                vv.scalar_tensor_tensor(x[:, 1], parts[:, 1], CW[:, 2:3], x[:, 1], ALU.mult,
                                        ALU.add).then_inc(v_xc, 1)

            def xcL(g):
                dve.wait_ge(a_xcH, g.n + 1)
                vv.scalar_tensor_tensor(XCL[:], XCP[:], 0.0, XCH[:].bitcast(F32), ALU.max,
                                        ALU.subtract).then_inc(v_xcL, 1)

            def ni(g):
                dve.wait_ge(a_q2, g.n + 1)
                dve.wait_ge(a_r, g.n + 1)
                vv.scalar_tensor_tensor(Q2[:], TR[:], 1.0, Q2[:], ALU.add, ALU.mult).then_inc(v_rq, 1)
                dve.wait_ge(v_rq, g.n + 1)
                vv.tensor_tensor(Q2[:], bank("in"), Q2[:], ALU.add).then_inc(v_ni, 1)

            def dh(g):
                dve.wait_ge(a_nn, g.n + 1)
                vv.tensor_tensor(DH[:], H1T[:, g.slot], Q2[:], ALU.subtract).then_inc(v_dh01, 1)
                dve.wait_ge(a_z, g.n + 1)
                dve.wait_ge(v_dh01, g.n * 2 + 1)
                vv.scalar_tensor_tensor(DH[:], TZ[:], 1.0, DH[:], ALU.add, ALU.mult).then_inc(v_dh01, 1)
                dve.wait_ge(v_dh01, g.n * 2 + 2)
                vv.scalar_tensor_tensor(DH[:], DH[:], 0.5, Q2[:], ALU.mult, ALU.add).then_inc(v_dh, 1)

            def x2(g):
                dve.wait_ge(pe_gruT, g.n + 1)
                vv.tensor_tensor(X2[:, g.slot % 2], bank("gruT"), X1[:, g.slot], ALU.add).then_inc(v_x2, 1)

            def bn2(g):
                dve.wait_ge(v_x2, g.n + 1)
                stats(2, g, X2[:, g.slot % 2]).then_inc(v_bn[2], 1)

            def add_bias(half):
                b = BANKS["hlB" if half else "hlA"]
                bias = ROWV[:, ROW_AT["L2_gnn_bl"]:ROW_AT["L2_gnn_bl"] + 3 * D].rearrange("p (w n) -> p w n", w=3)
                return vv.tensor_tensor(HLR[:, 2 * half:2 * half + 2, :, 0:D],
                                        PS[:, b:b + 2, 0:3 * D].rearrange("p g (w n) -> p g w n", w=3),
                                        bias.unsqueeze(1).to_broadcast([128, 2, 3, D]), ALU.add)

            def hleA(g):
                dve.wait_ge(pe_hlA, g.n + 1)
                add_bias(0).then_inc(v_hleA, 1)

            def hleB(g):
                dve.wait_ge(pe_hlB, g.n + 1)
                add_bias(1).then_inc(v_hleB, 1)

            def de(g):
                dve.wait_ge(a_sim, g.n + 1)
                vv.tensor_tensor(DE[:], EE[:], ADJT[:, g.slot], ALU.mult).then_inc(v_de, 1)

            def diag(g):
                dve.wait_ge(p_di, g.n + 1)
                vv.tensor_reduce(DG[:, g.slot % 2], EE[:], AX_X, ALU.add).then_inc(v_diag, 1)

            def cc(g):
                p = g.slot % 2
                wide = pair_wide("ctx", D + 1)
                dve.wait_ge(pe_ctx, g.n + 1)
                dve.wait_ge(p_hsd, g.n + 1)
                vv.tensor_tensor(DEN[:, 0, p], wide[:, :, D:D + 1].rearrange("p g o -> p (g o)"), DG[:, p],
                                 ALU.add).then_inc(v_den0, 1)
                vv.tensor_tensor(HSD[:], wide[:, :, 0:D], HSD[:], ALU.add).then_inc(v_cc, 1)
                dve.wait_ge(a_sim, g.n + 1)
                dve.wait_ge(v_den0, g.n + 1)
                vv.scalar_tensor_tensor(DEN[:, 1, p], ZS[:, p], L2_RENORM_EPS, DEN[:, 0, p], ALU.mult,
                                        ALU.add).then_inc(v_den, 1)

            def bn4(g):
                dve.wait_ge(v_cc, g.n + 1)
                stats(4, g, HSD).then_inc(v_bn[4], 1)

            def x3(g):
                dve.wait_ge(p_lnb, g.n + 1)
                vv.scalar_tensor_tensor(X3[:, g.slot % 2], CH[:], 0.0, X2[:, g.slot % 2], ALU.max,
                                        ALU.add).then_inc(v_x3, 1)

            def bn3(g):
                dve.wait_ge(v_x3, g.n + 1)
                stats(3, g, X3[:, g.slot % 2]).then_inc(v_bn[3], 1)

            def h3L(g):
                dve.wait_ge(a_h3H, g.n + 1)
                vv.tensor_tensor(H3L[:], bank("h3T"), H3H[:].bitcast(F32), ALU.subtract).then_inc(v_h3L, 1)

            def gp(g):
                dve.wait_ge(a_het, g.n + 1)
                vv.tensor_tensor(GP[:], pair_wide("hg", 2 * D)[:, :, D:2 * D], row("L3_gnn_b_t"), ALU.add).then_inc(v_gp, 1)

            def mix(g):
                dve.wait_ge(a_fh, g.n + 1)
                dve.wait_ge(a_het, g.n + 1)
                vv.tensor_tensor(FH[:], FH[:], HET[:], ALU.subtract).then_inc(v_mix01, 1)
                dve.wait_ge(a_gate, g.n + 1)
                dve.wait_ge(v_mix01, g.n * 2 + 1)
                vv.scalar_tensor_tensor(FH[:], GP[:], 1.0, FH[:], ALU.add, ALU.mult).then_inc(v_mix01, 1)
                dve.wait_ge(v_mix01, g.n * 2 + 2)
                vv.scalar_tensor_tensor(FH[:], FH[:], 0.5, HET[:], ALU.mult, ALU.add).then_inc(v_mix, 1)

            def out_(g):
                dve.wait_ge(a_ex, g.n + 1)
                dve.wait_ge(p_x3m, g.n + 1)
                vv.scalar_tensor_tensor(EX[:], EX[:], 1.0, X3M[:, g.slot % 2], ALU.min, ALU.add).then_inc(v_out0, 1)
                if g.has(2):
                    dve.wait_ge(out_stored[(g.slot + 2) % 4], (g.turn + (1 if g.slot >= 2 else 0)) * 16)
                dve.wait_ge(v_out0, g.n + 1)
                vv.scalar_tensor_tensor(OUT[:, g.slot % 2], FH[:], 0.0, EX[:], ALU.max, ALU.add).then_inc(v_out, 1)

            def one_step(turn, step):
                a, b, c, d, e = (group(turn, step, lag) for lag in range(LAGS))
                if c:
                    xc(c)
                if a:
                    deg(a)
                if e:
                    h3L(e)
                if c:
                    xcL(c)
                if a:
                    bn0(a)
                if d:
                    cc(d)
                    bn4(d)
                if c:
                    ni(c)
                if b:
                    s(b)
                    c1L(b)
                if c:
                    dh(c)
                if e:
                    gp(e)
                if c:
                    x2(c)
                    bn2(c)
                if b:
                    msgp(b)
                if e:
                    mix(e)
                if b:
                    xm(b)
                if d:
                    x3(d)
                    bn3(d)
                if a:
                    x1(a)
                    bn1(a)
                if c:
                    de(c)
                    hleA(c)
                if b:
                    nmL(b)
                if c:
                    hleB(c)
                if e:
                    out_(e)
                if c:
                    diag(c)

            schedule(dve, one_step)

        @block.tensor
        def _(pe):
            mm = nc.tensor.matmul

            def mm3(o, weight, hi, lo, start, stop):
                wh, wl = weight
                mm(o, wh, hi, start=start, stop=False)
                mm(o, wh, lo, start=False, stop=False)
                return mm(o, wl, hi, start=False, stop=stop)

            def transposes(name, src):
                for j in range(G):
                    last = nc.tensor.transpose(bank(name)[:, j], src[:, j], ident)
                return last

            def products(name, left, right):
                for j in range(G):
                    last = mm(bank(name)[:, j], left(j), right(j), start=True, stop=True)
                return last

            def conv1(g):
                if g.first:
                    pe.wait_ge(split_lo, stages_of("conv1"))
                if g.has(3):
                    pe.wait_ge(a_h3H, g.n - 2)
                if g.has(3):
                    pe.wait_ge(v_h3L, g.n - 2)
                pe.wait_ge(a_h1H, g.n + 1)
                pe.wait_ge(p_h1L, g.n + 1)
                mm3(whole("conv1"), w("conv1", 0), flat(H1H[:, g.slot]), flat(H1L[:, g.slot]), True,
                    True).then_inc(pe_conv1, 1)

            def msg(g):
                wide = pair_wide("msg", D + 3)
                if g.has(2):
                    pe.wait_ge(v_den, g.n - 1)
                pe.wait_ge(a_h1T, g.n + 1)
                for j in range(G):
                    last = mm(wide[:, j], H1T[:, g.slot, j], WMSG[:], start=True, stop=True)
                last.then_inc(pe_msg, 1)

            def gruH(g):
                h = (flat(H1H[:, g.slot]), flat(H1L[:, g.slot]))
                if g.first:
                    pe.wait_ge(split_lo, stages_of("whh"))
                if g.has(-1):
                    pe.wait_ge(a_yd, g.n + 2)
                if g.has(1):
                    pe.wait_ge(a_sim, g.n)
                if g.has(1):
                    pe.wait_ge(v_hleA, g.n)
                pe.wait_ge(p_h1L, g.n + 1)
                mm3(whole("hn"), w("whh", 2), *h, True, True).then_inc(pe_gruH, 1)
                mm3(whole("r"), w("whh", 0), *h, True, False)
                mm3(whole("z"), w("whh", 1), *h, True, False)

            def gruN(g):
                nm = (flat(NMH[:]), flat(NML[:]))
                if g.first:
                    pe.wait_ge(split_lo, stages_of("wih"))
                pe.wait_ge(a_nmH, g.n + 1)
                pe.wait_ge(v_nmL, g.n + 1)
                mm3(whole("r"), w("wih", 3), *nm, False, False)
                mm3(whole("z"), w("wih", 4), *nm, False, False)
                mm3(whole("in"), w("wih", 5), *nm, True, False).then_inc(pe_gruN, 1)

            def gruX(g):
                xc = (flat(XCH[:]), flat(XCL[:]))
                if g.first:
                    pe.wait_ge(split_lo, stages_of("wih"))
                pe.wait_ge(a_xcH, g.n + 1)
                pe.wait_ge(v_xcL, g.n + 1)
                mm3(whole("r"), w("wih", 0), *xc, False, True)
                mm3(whole("in"), w("wih", 2), *xc, False, True)
                mm3(whole("z"), w("wih", 1), *xc, False, True).then_inc(pe_gruX, 1)

            def u0(g):
                if g.has(1):
                    pe.wait_ge(v_msgp, g.n)
                pe.wait_ge(a_hp, g.n + 1)
                pe.wait_ge(p_adji, g.n + 1)
                products("u0", lambda j: HP[:, j], lambda j: ADJI[:, j]).then_inc(pe_u0, 1)

            def y0(g):
                pe.wait_ge(a_u0, g.n + 1)
                products("y0", lambda j: UT[:, j], lambda j: W0[:]).then_inc(pe_y0, 1)

            def h1T(g):
                if g.has(2):
                    pe.wait_ge(v_hleB, g.n - 1)
                pe.wait_ge(a_xh1, g.n + 1)
                transposes("h1T", XH1).then_inc(pe_h1T, 1)

            def sT(g):
                if g.has(1):
                    pe.wait_ge(a_z, g.n)
                pe.wait_ge(v_slr, g.n + 1)
                for side in (0, 1):
                    for j in range(G):
                        rows_of = SLR[:, j, side].bitcast(F32).rearrange("p b k -> p (b k)")
                        last = nc.tensor.transpose(PS[0:16, BANKS["sT"] + side, j * N:(j + 1) * N], rows_of, ident)
                last.then_inc(pe_sT, 1)

            def dist(g):
                pe.wait_ge(a_sT, g.n + 1)
                products("dist", lambda j: LRT[:, 0, j], lambda j: LRT[:, 1, j]).then_inc(pe_dist, 1)

            def nmp(g):
                pe.wait_ge(a_msg, g.n + 1)
                pe.wait_ge(p_at, g.n + 1)
                products("nmp", lambda j: MSG[:, j], lambda j: AT[:, j]).then_inc(pe_nmp, 1)

            def tap(k):
                return w("conv2", (k + 1) % TAPS)

            def tap_sum(j):
                return (SUMH[:, j * D:(j + 1) * D], SUML[:, j * D:(j + 1) * D]) if j < ODD else tap(2 * j)

            def cvM(g):
                o = whole("cvM")[:, 0:G * HALF].rearrange("p (g i) -> p g i", g=G)
                if g.first:
                    pe.wait_ge(split_lo, STAGES + 4)
                if g.has(3):
                    pe.wait_ge(v_gp, g.n - 2)
                pe.wait_ge(a_c1H, g.n + 1)
                pe.wait_ge(v_c1L, g.n + 1)
                for j in range(EVEN):
                    last = mm3(o, tap_sum(j), SH[:, 0, :, j:j + HALF], SL[:, 0, :, j:j + HALF], j == 0,
                               j == EVEN - 1)
                last.then_inc(pe_m, 1)

            halves = [(0, j) for j in range(EVEN)] + [(1, j) for j in range(ODD)]

            def conv2(g, part):
                parts = whole("conv2").rearrange("p (t g i) -> p t g i", t=2, g=G)
                for t, j in halves[part * SHARE:(part + 1) * SHARE]:
                    last = mm3(parts[:, t], tap(2 * j + t), SH[:, 1 + t, :, j:j + HALF],
                               SL[:, 1 + t, :, j:j + HALF], j == 0, j == (ODD if t else EVEN) - 1)
                return last

            def cv0(g):
                if g.first:
                    pe.wait_ge(split_lo, STAGES)
                pe.wait_ge(a_c1H, g.n + 1)
                pe.wait_ge(v_c1L, g.n + 1)
                conv2(g, 0)

            def cv5(g):
                conv2(g, 5).then_inc(pe_conv2, 1)

            def gruT(g):
                if g.has(-1):
                    pe.wait_ge(a_sT, g.n + 2)
                pe.wait_ge(v_dh, g.n + 1)
                transposes("gruT", DH).then_inc(pe_gruT, 1)

            def h2T(g):
                pe.wait_ge(a_xh2, g.n + 1)
                transposes("h2T", XH2).then_inc(pe_h2T, 1)

            def sim(g):
                pe.wait_ge(a_h2T, g.n + 1)
                products("sim", lambda j: H2T[:, j], lambda j: H2T[:, j]).then_inc(pe_sim, 1)

            def hl(g, half):
                wh, wl = w("wlsr", 0, 3)
                for j in (2 * half, 2 * half + 1):
                    o = PS[:, BANKS["hlB" if half else "hlA"] + j % 2, 0:3 * D]
                    mm(o, H2H[:, j], wh, start=True, stop=False)
                    mm(o, H2H[:, j], wl, start=False, stop=False)
                    last = mm(o, H2L[:, j], wh, start=False, stop=True)
                return last

            def hlA(g):
                if g.first:
                    pe.wait_ge(split_lo, stages_of("wlsr"))
                if g.has(-2):
                    pe.wait_ge(a_yd, g.n + 3)
                pe.wait_ge(p_h2L, g.n + 1)
                hl(g, 0).then_inc(pe_hlA, 1)

            def hlB(g):
                if g.first:
                    pe.wait_ge(split_lo, stages_of("wlsr"))
                pe.wait_ge(p_h2L, g.n + 1)
                hl(g, 1).then_inc(pe_hlB, 1)

            def ctx_(g):
                wide = pair_wide("ctx", D + 1)
                if g.has(-2):
                    pe.wait_ge(a_h1T, g.n + 3)
                pe.wait_ge(p_dl, g.n + 1)
                pe.wait_ge(v_hleA, g.n + 1)
                pe.wait_ge(v_hleB, g.n + 1)
                for j in range(G):
                    mm(wide[:, j], DL[:, j], HLR[:, j, 0, 0:D + 1], start=True, stop=False)
                    last = mm(wide[:, j], DR[:, j], HLR[:, j, 2, 0:D + 1], start=False, stop=True)
                last.then_inc(pe_ctx, 1)

            def h3T(g):
                if g.has(-2):
                    pe.wait_ge(v_nmL, g.n + 3)
                pe.wait_ge(a_xh3, g.n + 1)
                transposes("h3T", XH3).then_inc(pe_h3T, 1)

            def g3(g):
                if g.has(-3):
                    pe.wait_ge(a_c1, g.n + 4)
                pe.wait_ge(a_h3H, g.n + 1)
                pe.wait_ge(v_h3L, g.n + 1)
                pe.wait_ge(a_hn3, g.n + 1)
                products("g3", lambda j: HN[:, j], lambda j: ADJT[:, g.slot, j]).then_inc(pe_g3, 1)

            def fhom(g):
                pe.wait_ge(a_g3, g.n + 1)
                products("fhom", lambda j: G3T[:, j], lambda j: THETA[:]).then_inc(pe_fhom, 1)

            def hg(g):
                wh, wl = w("whet", 0, 2)
                wide = pair_wide("hg", 2 * D)
                if g.first:
                    pe.wait_ge(split_lo, stages_of("whet"))
                if g.has(-2):
                    pe.wait_ge(a_z, g.n + 3)
                if g.has(-2):
                    pe.wait_ge(v_ni, g.n + 3)
                pe.wait_ge(a_h3H, g.n + 1)
                pe.wait_ge(v_h3L, g.n + 1)
                for j in range(G):
                    mm(wide[:, j], H3H[:, j], wh, start=True, stop=False)
                    mm(wide[:, j], H3H[:, j], wl, start=False, stop=False)
                    last = mm(wide[:, j], H3L[:, j], wh, start=False, stop=True)
                last.then_inc(pe_hg, 1)

            pe.wait_ge(consts_in, 48)
            pe.wait_ge(weights_in, 48)

            def one_step(turn, step):
                a, b, c, d, e = (group(turn, step, lag) for lag in range(LAGS))
                if c:
                    cv5(c)
                    gruH(c)
                if e:
                    h3T(e)
                if b:
                    h1T(b)
                if c:
                    gruN(c)
                if d:
                    ctx_(d)
                if b:
                    conv1(b)
                if c:
                    gruX(c)
                if e:
                    g3(e)
                if b:
                    msg(b)
                if e:
                    fhom(e)
                    hg(e)
                if b:
                    sT(b)
                    cv0(b)
                    conv2(b, 1)
                if c:
                    gruT(c)
                if b:
                    dist(b)
                    cvM(b)
                    conv2(b, 2)
                if a:
                    u0(a)
                if b:
                    conv2(b, 3)
                if c:
                    h2T(c)
                if a:
                    y0(a)
                if b:
                    nmp(b)
                if c:
                    sim(c)
                if b:
                    conv2(b, 4)
                if c:
                    hlA(c)
                    hlB(c)

            schedule(pe, one_step)


def kernel(**inputs):
    import concourse.bacc as bacc
    from concourse.bass_utils import run_bass_kernel_spmd

    def arr(name):
        return np.asarray(inputs[name])

    m, n = np.arange(N)[:, None], np.arange(N)[None, :]
    eye = np.ascontiguousarray(np.stack([m == n, m > n, m < n], axis=1).astype(np.float32))
    bih, bhh = arr("L1_gnn_b_ih").reshape(3, D), arr("L1_gnn_b_hh").reshape(3, D)
    split = {
        "conv1": arr("L1_gnn_conv1_w")[:, :, 0].T,
        "whh": arr("L1_gnn_w_hh").T,
        "wih": arr("L1_gnn_w_ih").T.reshape(2, D, 3 * D).transpose(1, 0, 2).reshape(D, 6 * D),
        "whet": np.concatenate([arr("L3_gnn_W_h"), arr("L3_gnn_W_t")], axis=1),
        "wlsr": np.concatenate([arr("L2_gnn_Wl"), arr("L2_gnn_Ws"), arr("L2_gnn_Wr")]).T,
        "conv2": np.roll(arr("L1_gnn_conv2_w").transpose(1, 2, 0), 1, axis=1).reshape(D, TAPS * D),
    }
    arrays = {
        "x": arr("x"),
        "adj": arr("adj"),
        "adjT": np.ascontiguousarray(arr("adj").transpose(0, 2, 1)),
        "eye": eye,
        "rows": np.concatenate([arr(r) for r in ROWS]),
        "cols": np.ascontiguousarray(np.stack(
            [arr("L1_gnn_" + c) for c in COLS[:8]] + [bih[0], bih[1], bih[2], bhh[0], bhh[1], bhh[2]], axis=1)),
        "w0": arr("L0_gnn_W"),
        "wmsgT": np.ascontiguousarray(np.concatenate([arr("L1_gnn_w_msg"), arr("L1_gnn_w_se")]).T),
        "theta": arr("L3_gnn_theta"),
        "split_w": np.concatenate([split[name] for name in SPLIT], axis=1),
    }
    nc = bacc.Bacc("TRN2", target_bir_lowering=False, num_devices=1)
    args, feeds = [], {}
    for name, a in arrays.items():
        feeds[f"in_{name}"] = a
        args.append(nc.dram_tensor(f"in_{name}", a.shape, F32, kind="ExternalInput").ap())
    args.append(nc.dram_tensor("out_0", (B, N, D), F32, kind="ExternalOutput").ap())
    build(nc, *args)
    r = run_bass_kernel_spmd(nc, [feeds], core_ids=[0])
    return r.results[0]["out_0"]
```
